# Optimizing a Trainium2 kernel written in Bass

```python
import numpy as np
import jax
import jax.numpy as jnp

def _softmax(x, axis=-1):
    return jax.nn.softmax(x, axis=axis)

def _gelu(x):
    return jax.nn.gelu(x, approximate=True)

def _silu(x):
    return jax.nn.silu(x)

def _sigmoid(x):
    return jax.nn.sigmoid(x)

def _layernorm(x, axis=-1, eps=1e-05):
    m = jnp.mean(x, axis=axis, keepdims=True)
    v = jnp.var(x, axis=axis, keepdims=True)
    return (x - m) / jnp.sqrt(v + eps)

def _scatter_add(tgt, idx, src, axis=0):
    return tgt.at[idx].add(src)

def _segment_sum(src, seg, n):
    return jax.ops.segment_sum(src, seg, n)
kernel_name = 'mk_gnn_preln_d1_gnn_r8_6dfd7c'

def setup_inputs(seed: int=0):
    np.random.seed(seed)
    _w = jnp.asarray

    def _rec_inputs():
        import jax
        import jax.numpy as jnp
        _gk = jax.random.key(seed)
        x = -0.000202 + 1 * jax.random.normal(jax.random.fold_in(_gk, 1), (6250, 128), jnp.float32)
        _s = jax.random.randint(jax.random.fold_in(_gk, 2), (50000,), 0, 6250, jnp.int32)
        _d = jax.random.randint(jax.random.fold_in(_gk, 3), (50000,), 0, 6250, jnp.int32)
        _loop = jnp.arange(6250, dtype=jnp.int32)
        src = jnp.concatenate([_s, _d, _loop])
        dst = jnp.concatenate([_d, _s, _loop])
        _o = jnp.argsort(dst, stable=True)
        src = src[_o]
        dst = dst[_o]
        edge_weight = jax.random.uniform(jax.random.fold_in(_gk, 12), (106250,), jnp.float32, 0.0, 1)
        return (x, src, dst, edge_weight)
    x, src, dst, edge_weight = _rec_inputs()

    def _L0_gnn_setup():
        import jax, jax.numpy as jnp
        import numpy as np
        N_NODES = 6250
        N_EDGES = 100000
        HID = 128
        key = jax.random.key(seed)
        ks = jax.random.split(key, 10)
        s_msg = 1.0 / np.sqrt(2 * HID + 1)
        s_u1 = 1.0 / np.sqrt(2 * HID)
        s_u2 = 1.0 / np.sqrt(HID)
        return {'z': jax.random.normal(ks[0], (N_NODES, HID), dtype=jnp.float32), 'edge_weight': jax.random.uniform(ks[1], (N_EDGES,), dtype=jnp.float32), 'edge_src': jax.random.randint(ks[2], (N_EDGES,), 0, N_NODES), 'edge_dst': jax.random.randint(ks[3], (N_EDGES,), 0, N_NODES), 'Wm': jax.random.normal(ks[4], (2 * HID + 1, HID), dtype=jnp.float32) * s_msg, 'bm': jax.random.normal(ks[5], (HID,), dtype=jnp.float32) * s_msg, 'W1': jax.random.normal(ks[6], (2 * HID, HID), dtype=jnp.float32) * s_u1, 'b1': jax.random.normal(ks[7], (HID,), dtype=jnp.float32) * s_u1, 'W2': jax.random.normal(ks[8], (HID, HID), dtype=jnp.float32) * s_u2, 'b2': jax.random.normal(ks[9], (HID,), dtype=jnp.float32) * s_u2}
    _L0_gnn_all = _L0_gnn_setup()
    _L0_gnn_in = {k: v for k, v in _L0_gnn_all.items() if k in ('Wm', 'bm', 'W1', 'b1', 'W2', 'b2')}
    del _L0_gnn_all
    return {'x': x, 'src': src, 'dst': dst, 'edge_weight': edge_weight, 'L0_gnn_Wm': _L0_gnn_in['Wm'], 'L0_gnn_bm': _L0_gnn_in['bm'], 'L0_gnn_W1': _L0_gnn_in['W1'], 'L0_gnn_b1': _L0_gnn_in['b1'], 'L0_gnn_W2': _L0_gnn_in['W2'], 'L0_gnn_b2': _L0_gnn_in['b2']}

def reference(x, src, dst, edge_weight, L0_gnn_Wm, L0_gnn_bm, L0_gnn_W1, L0_gnn_b1, L0_gnn_W2, L0_gnn_b2):
    import jax
    import jax.numpy as jnp

    def _L0_gnn_ref(z, edge_weight, edge_src, edge_dst, Wm, bm, W1, b1, W2, b2):
        import jax, jax.numpy as jnp
        import numpy as np
        N_NODES = 6250
        N_EDGES = 100000
        HID = 128
        n, H = z.shape
        Wd, Ws, ww = (Wm[:H], Wm[H:2 * H], Wm[2 * H])
        msgs = z[edge_dst] @ Wd + z[edge_src] @ Ws + edge_weight[:, None] * ww[None, :] + bm
        agg = jax.ops.segment_max(msgs, edge_dst, num_segments=n)
        deg = jax.ops.segment_sum(jnp.ones_like(edge_weight), edge_dst, num_segments=n)
        agg = jnp.where(deg[:, None] > 0, agg, jnp.zeros((), dtype=z.dtype))
        W1a, W1b = (W1[:H], W1[H:])
        hidden = jax.nn.relu(z @ W1a + agg @ W1b + b1)
        return hidden @ W2 + b2
    h = jnp.maximum(_layernorm(x, axis=-1), 0.0)
    x = x + _L0_gnn_ref(h, edge_weight, src, dst, L0_gnn_Wm, L0_gnn_bm, L0_gnn_W1, L0_gnn_b1, L0_gnn_W2, L0_gnn_b2)
    return x

_drawn_inputs = setup_inputs


def setup_inputs(seed=0):
    import zlib

    import numpy as np

    out = dict(_drawn_inputs(seed))
    spreads = {}
    factors = {'edge_weight': 7.744}
    for name, (base, spread) in spreads.items():
        noise = np.random.default_rng([zlib.crc32(name.encode()), seed]).standard_normal(out[name].shape)
        drawn = base * np.exp(spread * noise) if base else spread * noise
        out[name] = jnp.asarray(drawn.astype(out[name].dtype))
    for name, factor in factors.items():
        out[name] = (out[name] * factor).astype(out[name].dtype)
    return out
```

```python
from contextlib import ExitStack

import concourse.bass as bass
from concourse import mybir

F32 = mybir.dt.float32
I32 = mybir.dt.int32
ALU = mybir.AluOpType
ACT = mybir.ActivationFunctionType

P = 128
D = 128
N_NODES = 6250
N_EDGES = 106250
NT = -(-N_NODES // P)
NN = P * NT
G = 8
SLOTS = 4
PER_LOOP = G * SLOTS
CH = -(-N_EDGES // (P * PER_LOOP)) * PER_LOOP
NE = P * CH
LOOPS = CH // PER_LOOP
ROW = 256
HEADS = NE // ROW
SB_ = 10
NS = NT + 1
NSB = NS // SB_
TG = 7
NTG = NT // TG
UG = 4
NUG = -(-NT // UG)
LAST_UG = NT - (NUG - 1) * UG
LIMIT = 3.4028234663852886e38
HUGE = 2.0 ** 127
EPS = 1e-5
OPS = 2 * G
assert NT % TG == 0 and NE % ROW == 0 and NS % SB_ == 0 and NTG % 2 == 1 and NUG % 2 == 1


def build(nc, x, src, dst, ew, Wm, bm, W1, b1, W2, b2, q_tab, m_tab, out):
    ctx = ExitStack()
    with ctx:
        def sb(name, shape, dt=F32):
            return ctx.enter_context(nc.sbuf_tensor(name, shape, dt))

        def sem(name):
            return ctx.enter_context(nc.semaphore(name))

        xs = sb("xs", [P, NT, D])
        hT = sb("hT", [P, NT * P])
        pm = sb("pm", [P, NT, D])
        rows = sb("rows", [P, NS, ROW], I32)
        src_sb = sb("src_sb", [P, CH], I32)
        dst_sb = sb("dst_sb", [P, CH], I32)
        w_sb = sb("w_sb", [P, CH])
        keep = sb("keep", [P, CH])
        gath = sb("gath", [P, SLOTS, G, D])
        runm = sb("runm", [P, SLOTS, G, D])
        xn = gath[:, 0:2, 0:TG, :]
        hring = runm[:, 0:2, 0:TG, :].rearrange("p s t f -> p s (t f)")
        q_sb = runm[:, 2, 0:TG, :]
        ident = sb("ident", [P, P])
        wsd = sb("wsd", [P, 2 * D])
        w1a = sb("w1a", [P, D])
        w1b = sb("w1b", [P, D])
        w2 = sb("w2", [P, D])
        ww_b = sb("ww_b", [P, D])
        b2_b = sb("b2_b", [P, D])
        bm_b = sb("bm_b", [P, D])
        b1_col = sb("b1_col", [P, 1])
        ones = sb("ones", [P, ROW])
        minus_huge = sb("minus_huge", [1, 1])
        head_row = sb("head_row", [1, HEADS], I32)
        head_f = sb("head_f", [1, HEADS])
        heads = sb("heads", [P, HEADS])
        node_id = sb("node_id", [P, NS])
        tile_step = sb("tile_step", [P, P])
        minus_t = sb("minus_t", [P, NT])
        junk = sb("junk", [P, 2, HEADS])
        cnt = sb("cnt", [P, NS])
        cnt2 = sb("cnt2", [P, NS])
        row_f = sb("row_f", [P, NS])
        row_i = sb("row_i", [P, NS], I32)
        src_idx = sb("src_idx", [P, 2, PER_LOOP // 2], I32)
        last_idx = sb("last_idx", [P, 2, UG], I32)
        last_f = sb("last_f", [P, NS])
        last_i = sb("last_i", [P, NS], I32)
        has = sb("has", [P, NT])
        stats = sb("stats", [P, NT, 6])
        mean = sb("mean", [P, NT])
        diff = sb("diff", [P, NT])
        var = sb("var", [P, NT])
        std = sb("std", [P, NT])
        rstd = sb("rstd", [P, NT])
        eps_col = sb("eps_col", [P, 1])
        ends = sb("ends", [P, 4], I32)
        ends_f = sb("ends_f", [P, 4])
        flag = sb("flag", [P, 4])
        key_t = sb("key_t", [P, NT])
        cmask = sb("cmask", [P, P])
        cmask_T = sb("cmask_T", [P, P])
        ct = sb("ct", [P, P + 1])
        cprev = sb("cprev", [P, D])
        huge_col = sb("huge_col", [P, 1])
        spare = rows[:, :, :].rearrange("p s r -> p (s r)").bitcast(F32)
        spare = spare[:, 0:8 * UG * D].rearrange("p (n j f) -> p n j f", n=8, f=D)
        onehot = spare[:, 0, :, :]
        mmax = spare[:, 1, :, :]
        agg = spare[:, 2:4, :, :]
        aggT = spare[:, 4:6, :, :].rearrange("p s j f -> p s (j f)")
        hidT = spare[:, 6:8, :, :].rearrange("p s j f -> p s (j f)")

        ps = ctx.enter_context(nc.psum_tensor("ps", [P, 8, 512], F32))
        ps_xT = [ps[:, 2 * i:2 * i + 2, :].rearrange("p b c -> p (b c)") for i in range(2)]
        ps_qp = ps[:, 4:8, :].rearrange("p b c -> p (b c)").rearrange("p (t c) -> p t c", c=2 * D)
        ps_heads = ps[:, 0, 0:HEADS]
        ps_cmask = ps[:, 1, 0:P]
        ps_F = ps[:, 2, 0:P]
        ps_C = ps[:, 3, 0:P]
        ps_fix = ps[:, 0, :].rearrange("p (j f) -> p j f", f=D)
        ps_neg = ps[:, 1, 0:UG]
        ps_aggT = [ps[:, 2 + i, :] for i in range(2)]
        ps_hid = [ps[:, 4 + i, :] for i in range(2)]
        ps_out = [ps[:, 6 + i, :].rearrange("p (j f) -> p j f", f=D) for i in range(2)]

        const_made = sem("const_made")
        ident_zero = sem("ident_zero")
        ends_clear = sem("ends_clear")
        head_in = sem("head_in")
        x_in = sem("x_in")
        weights_in = sem("weights_in")
        edges_in = sem("edges_in")
        ends_in = sem("ends_in")
        heads_spread = sem("heads_spread")
        counted = sem("counted")
        row_ready = sem("row_ready")
        rows_in = [sem(f"rows_in{i}") for i in range(NSB)]
        src_idx_made = [sem(f"src_idx_made{i}") for i in range(2)]
        last_idx_made = sem("last_idx_made")
        std_made = sem("std_made")
        normed = sem("normed")
        xT_made = sem("xT_made")
        h_made = sem("h_made")
        h_kept = [sem(f"h_kept{i}") for i in range(2)]
        qp_made = sem("qp_made")
        q_taken = sem("q_taken")
        p_taken = sem("p_taken")
        q_stored = sem("q_stored")
        edge_step = sem("edge_step")
        gathered = [sem(f"gathered{i}") for i in range(SLOTS)]
        m_stored = [sem(f"m_stored{i}") for i in range(SLOTS)]
        cmask_spread = sem("cmask_spread")
        F_turned = sem("F_turned")
        carry_step = sem("carry_step")
        C_turned = sem("C_turned")
        carry_ready = sem("carry_ready")
        onehot_made = sem("onehot_made")
        fix_made = sem("fix_made")
        m_gathered = [[sem(f"m_gathered{s}_{j}") for j in range(UG)] for s in range(2)]
        joined = sem("joined")
        agg_made = sem("agg_made")
        aggT_made = sem("aggT_made")
        aggT_kept = sem("aggT_kept")
        hid_made = sem("hid_made")
        hid_kept = sem("hid_kept")
        out_made = sem("out_made")
        res_made = sem("res_made")
        res_stored = sem("res_stored")
        block = ctx.enter_context(nc.Block())

        stat_step = sem("stat_step")
        var_made = sem("var_made")
        rstd_made = sem("rstd_made")
        prep = sem("prep")
        cmask_made = sem("cmask_made")
        last_made = sem("last_made")
        m_rows = m_tab.rearrange("(p j) f -> p j f", p=P)
        q_rows = q_tab.rearrange("(p t) f -> p t f", p=P)
        out_rows = out.rearrange("(p t) f -> p t f", p=P)
        CONSTS = 11
        WEIGHTS = 9

        def over_tiles(row):
            return row[:, :].rearrange("p (t f) -> p t f", t=1).broadcast_to([P, NT, D])

        @block.sync
        def _(sp):
            with nc.allow_non_contiguous_dma(reason="one entry of each row"):
                sp.dma_start(head_row[:, :], dst.rearrange("(a r) -> a r", r=ROW)[:, 0:1].rearrange(
                    "a r -> r a")).then_inc(head_in, 16)
            sp.dma_start(xs[:, :, :], x.rearrange("(p t) f -> p t f", p=P)).then_inc(x_in, 16)
            sp.dma_start(src_sb[:, :], src.rearrange("(p j) -> p j", p=P)).then_inc(edges_in, 16)
            sp.dma_start(dst_sb[:, :], dst.rearrange("(p j) -> p j", p=P)).then_inc(edges_in, 16)
            sp.dma_start(w_sb[:, :], ew.rearrange("(p j) -> p j", p=P)).then_inc(edges_in, 16)

            def table_group(g, slot):
                sp.wait_ge(h_made, g + 1)
                sp.dma_start(hT[:, bass.ds(g * (TG * P), TG * P)], hring[:, slot, :]).then_inc(h_kept[slot], 16)
                sp.wait_ge(q_taken, g + 1)
                sp.dma_start(q_rows[:, bass.ds(g * TG, TG), :], q_sb[:, :, :]).then_inc(q_stored, 16)

            with sp.Fori(0, NTG // 2) as i:
                table_group(2 * i, 0)
                table_group(2 * i + 1, 1)
            table_group(NTG - 1, 0)

            with sp.Fori(0, LOOPS) as i:
                for s in range(SLOTS):
                    sp.wait_ge(edge_step, i * (OPS * SLOTS) + OPS * (s + 1))
                    sp.dma_start(m_rows[:, bass.ds(i * PER_LOOP + s * G, G), :],
                                 runm[:, s, :, :]).then_inc(m_stored[s], 16)

            def update_group(g, n):
                sp.wait_ge(res_made, g + 1)
                sp.dma_start(out_rows[:, bass.ds(g * UG, n), :],
                             xs[:, bass.ds(g * UG, n), :]).then_inc(res_stored, 16)

            with sp.Fori(0, NUG - 1) as g:
                update_group(g, UG)
            update_group(NUG - 1, LAST_UG)
            sp.wait_ge(res_stored, 16 * NUG)

        @block.gpsimd
        def _(pool):
            pool.iota(node_id[:, :], [[1, NS]], base=-1, channel_multiplier=NT,
                      allow_small_or_imprecise_dtypes=True).then_inc(const_made, 1)
            pool.memset(ones[:, :], 1.0).then_inc(const_made, 1)
            pool.memset(ends[:, :], -1).then_inc(ends_clear, 1)
            pool.memset(eps_col[:, :], EPS).then_inc(const_made, 1)
            pool.memset(ident[:, :], 0.0).then_inc(ident_zero, 1)
            pool.wait_ge(ident_zero, 1)
            pool.affine_select(out=ident[:, :], in_=ident[:, :], compare_op=ALU.not_equal, fill=1.0, base=0,
                               pattern=[[-1, P]], channel_multiplier=1).then_inc(const_made, 1)
            pool.iota(tile_step[:, :], [[NT, P]], base=0, channel_multiplier=0,
                      allow_small_or_imprecise_dtypes=True).then_inc(const_made, 1)
            pool.iota(minus_t[:, :], [[-1, NT]], base=0, channel_multiplier=0,
                      allow_small_or_imprecise_dtypes=True).then_inc(const_made, 1)
            pool.memset(minus_huge[:, :], -HUGE).then_inc(const_made, 1)
            pool.memset(keep[:, 0:1], -LIMIT).then_inc(const_made, 1)
            pool.memset(runm[:, SLOTS - 1, G - 1, :], 0.0).then_inc(const_made, 1)
            pool.memset(ct[:, 0:1], 0.0).then_inc(const_made, 1)
            pool.memset(huge_col[:, :], HUGE).then_inc(const_made, 1)

            dst_rows = dst.rearrange("(a r) -> a r", r=ROW)
            for b in range(NSB):
                pool.wait_ge(row_ready, b + 1)
                for s in range(b * SB_, (b + 1) * SB_):
                    pool.indirect_dma_start(rows[:, s, :], None, dst_rows,
                                            bass.IndirectOffsetOnAxis(row_i[:, s:s + 1], 0)).then_inc(rows_in[b], 16)

            pool.wait_ge(q_stored, 16 * NTG)

            def gather_group(i, s):
                pool.wait_ge(src_idx_made[s // 2], i + 1)
                pool.nop(nofuse=True)
                for j in range(G):
                    pool.indirect_dma_start(gath[:, s, j, :], None, q_tab,
                                            bass.IndirectOffsetOnAxis(
                                                src_idx[:, s // 2, s % 2 * G + j:s % 2 * G + j + 1], 0)
                                            ).then_inc(gathered[s], 16)

            for s in range(SLOTS):
                gather_group(0, s)
            with pool.Fori(1, LOOPS) as i:
                for s in range(SLOTS):
                    pool.wait_ge(edge_step, (i - 1) * (OPS * SLOTS) + OPS * (s + 1))
                    pool.nop(nofuse=True)
                    gather_group(i, s)

            for s in range(SLOTS):
                pool.wait_ge(m_stored[s], 16 * LOOPS)
            pool.wait_ge(last_made, 1)
            pool.wait_ge(edge_step, OPS * SLOTS * LOOPS)

            def update_group(g, slot, n, wait):
                if wait:
                    pool.wait_ge(joined, (g - 1) * UG)
                pool.tensor_copy(last_idx[:, slot, 0:n], last_i[:, bass.ds(g * UG + 1, n)]).then_inc(last_idx_made, 1)
                pool.wait_ge(last_idx_made, g + 1)
                pool.nop(nofuse=True)
                for j in range(n):
                    pool.indirect_dma_start(gath[:, slot, j, :], None, m_tab,
                                            bass.IndirectOffsetOnAxis(last_idx[:, slot, j:j + 1], 0)
                                            ).then_inc(m_gathered[slot][j], 16)

            update_group(0, 0, UG, False)
            update_group(1, 1, UG, False)
            with pool.Fori(1, NUG // 2) as i:
                update_group(2 * i, 0, UG, True)
                update_group(2 * i + 1, 1, UG, True)
            update_group(NUG - 1, 0, LAST_UG, True)

        @block.scalar
        def _(act):
            act.dma_start(wsd[:, 0:D], Wm[D:2 * D, :]).then_inc(weights_in, 16)
            act.dma_start(wsd[:, D:2 * D], Wm[0:D, :]).then_inc(weights_in, 16)
            act.dma_start(w1a[:, :], W1[0:D, :]).then_inc(weights_in, 16)
            act.dma_start(w1b[:, :], W1[D:2 * D, :]).then_inc(weights_in, 16)
            act.dma_start(w2[:, :], W2).then_inc(weights_in, 16)
            act.dma_start(ww_b[:, :], Wm[2 * D:2 * D + 1, :].broadcast_to([P, D])).then_inc(weights_in, 16)
            act.dma_start(b2_b[:, :], b2.rearrange("(a f) -> a f", a=1).broadcast_to([P, D])).then_inc(weights_in, 16)
            act.dma_start(bm_b[:, :], bm.rearrange("(a f) -> a f", a=1).broadcast_to([P, D])).then_inc(weights_in, 16)
            with nc.allow_non_contiguous_dma(reason="a bias for each partition"):
                act.dma_start(b1_col[:, :], b1.rearrange("(f a) -> f a", a=1)).then_inc(weights_in, 16)
            act.wait_ge(ends_clear, 1)
            dst_pj = dst.rearrange("(p j) -> p j", p=P)
            with nc.allow_non_contiguous_dma(reason="one entry of each partition's edges"):
                act.dma_start(ends[:, 0:1], dst_pj[:, 0:1]).then_inc(ends_in, 16)
                act.dma_start(ends[:, 1:2], dst_pj[:, CH - 1:CH]).then_inc(ends_in, 16)
                act.dma_start(ends[1:P, 2:3], dst_pj[0:P - 1, CH - 1:CH]).then_inc(ends_in, 16)
                act.dma_start(ends[0:P - 1, 3:4], dst_pj[1:P, 0:1]).then_inc(ends_in, 16)

            act.wait_ge(const_made, CONSTS)
            act.wait_ge(var_made, 1)
            nc.scalar.activation(std[:, :], var[:, :], ACT.Sqrt, bias=eps_col[:, 0:1]).then_inc(std_made, 1)

            def table_group(i, slot, first):
                g = 2 * i + slot
                act.wait_ge(xT_made, g + 1)
                if not first:
                    act.wait_ge(h_kept[slot], 16 * i)
                    act.wait_ge(qp_made, g - 1)
                nc.scalar.activation(hring[:, slot, :], ps_xT[slot][:, 0:TG * P], ACT.Relu).then_inc(h_made, 1)
                act.wait_ge(qp_made, g + 1)
                if not first or slot:
                    act.wait_ge(q_stored, g * 16)
                nc.scalar.copy(q_sb[:, :, :], ps_qp[:, 0:TG, 0:D]).then_inc(q_taken, 1)
                nc.scalar.copy(pm[:, bass.ds(g * TG, TG), :], ps_qp[:, 0:TG, D:2 * D]).then_inc(p_taken, 1)

            table_group(0, 0, True)
            table_group(0, 1, True)
            with act.Fori(1, NTG // 2) as i:
                table_group(i, 0, False)
                table_group(i, 1, False)
            table_group(NTG // 2, 0, False)

            act.wait_ge(edges_in, 48)
            def indices(i, first):
                for half in range(2):
                    if not first:
                        act.wait_ge(gathered[2 * half], 16 * G * i)
                        act.wait_ge(gathered[2 * half + 1], 16 * G * i)
                    nc.scalar.copy(src_idx[:, half, :],
                                   src_sb[:, bass.ds(i * PER_LOOP + half * (PER_LOOP // 2), PER_LOOP // 2)]
                                   ).then_inc(src_idx_made[half], 1)

            indices(0, True)
            with act.Fori(1, LOOPS) as i:
                indices(i, False)

            def update_group(g, slot, n, wait):
                act.wait_ge(aggT_made, g + 1)
                if wait:
                    act.wait_ge(hid_made, g - 1)
                nc.scalar.copy(aggT[:, slot, 0:n * P], ps_aggT[slot][:, 0:n * P]).then_inc(aggT_kept, 1)
                act.wait_ge(hid_made, g + 1)
                if wait:
                    act.wait_ge(out_made, g - 1)
                nc.scalar.activation(hidT[:, slot, 0:n * P], ps_hid[slot][:, 0:n * P], ACT.Relu,
                                     bias=b1_col[:, 0:1]).then_inc(hid_kept, 1)

            update_group(0, 0, UG, False)
            update_group(1, 1, UG, False)
            with act.Fori(1, NUG // 2) as i:
                update_group(2 * i, 0, UG, True)
                update_group(2 * i + 1, 1, UG, True)
            update_group(NUG - 1, 0, LAST_UG, True)

        @block.vector
        def _(dve):
            dve.wait_ge(head_in, 16)
            nc.vector.tensor_copy(head_f[:, :], head_row[:, :]).then_inc(counted, 1)
            dve.wait_ge(heads_spread, 1)
            nc.vector.tensor_copy(heads[:, :], ps_heads).then_inc(counted, 1)
            dve.wait_ge(counted, 2)
            dve.wait_ge(const_made, CONSTS)
            with dve.Fori(0, NSB) as b:
                for j in range(SB_):
                    s = b * SB_ + j
                    dve.wait_ge(counted, s + 1)
                    nc.vector.tensor_scalar(junk[:, j % 2, :], heads[:, :], node_id[:, bass.ds(s, 1)], None,
                                            ALU.is_le, ALU.add, accum_out=cnt[:, bass.ds(s, 1)]
                                            ).then_inc(counted, 1)
                dve.wait_ge(counted, (b + 1) * SB_ + 2)
                nc.vector.tensor_scalar(row_i[:, bass.ds(b * SB_, SB_)], cnt[:, bass.ds(b * SB_, SB_)], -1.0, 0.0,
                                        ALU.add, ALU.max).then_inc(row_ready, 1)
            nc.vector.tensor_scalar(row_f[:, :], cnt[:, :], -1.0, 0.0, ALU.add, ALU.max).then_inc(counted, 1)

            dve.wait_ge(x_in, 16)
            with dve.Fori(0, NT // TG) as g:
                for j in range(TG):
                    nc.vector.bn_stats(stats[:, bass.ds(g * TG + j, 1), :].rearrange("p a c -> p (a c)"),
                                       xs[:, bass.ds(g * TG + j, 1), :].rearrange("p a f -> p (a f)")
                                       ).then_inc(stat_step, 1)
            dve.wait_ge(stat_step, NT)
            nc.vector.tensor_tensor(mean[:, :], stats[:, :, 1], stats[:, :, 4], ALU.add).then_inc(stat_step, 1)
            nc.vector.tensor_tensor(diff[:, :], stats[:, :, 1], stats[:, :, 4], ALU.subtract).then_inc(stat_step, 1)
            nc.vector.tensor_tensor(var[:, :], stats[:, :, 2], stats[:, :, 5], ALU.add).then_inc(stat_step, 1)
            dve.wait_ge(stat_step, NT + 2)
            nc.vector.scalar_tensor_tensor(out=diff[:, :], in0=diff[:, :], scalar=0.25, in1=diff[:, :],
                                           op0=ALU.mult, op1=ALU.mult).then_inc(stat_step, 1)
            nc.vector.tensor_scalar(mean[:, :], mean[:, :], 0.5, None, ALU.mult).then_inc(stat_step, 1)
            dve.wait_ge(stat_step, NT + 4)
            nc.vector.scalar_tensor_tensor(out=var[:, :], in0=var[:, :], scalar=1.0 / D, in1=diff[:, :],
                                           op0=ALU.mult, op1=ALU.add).then_inc(var_made, 1)
            dve.wait_ge(std_made, 1)
            nc.vector.reciprocal(rstd[:, :], std[:, :]).then_inc(rstd_made, 1)
            dve.wait_ge(rstd_made, 1)

            def norm_group(g, slot, wait):
                if wait:
                    dve.wait_ge(xT_made, g - 1)
                for j in range(TG):
                    t = g * TG + j
                    nc.vector.tensor_scalar(xn[:, slot, j, :], xs[:, bass.ds(t, 1), :].rearrange("p a f -> p (a f)"),
                                            mean[:, bass.ds(t, 1)],
                                            rstd[:, bass.ds(t, 1)], ALU.subtract, ALU.mult).then_inc(normed, 1)

            norm_group(0, 0, False)
            norm_group(1, 1, False)
            with dve.Fori(1, NTG // 2) as i:
                norm_group(2 * i, 0, True)
                norm_group(2 * i + 1, 1, True)
            norm_group(NTG - 1, 0, True)

            dve.wait_ge(weights_in, 16 * WEIGHTS)
            dve.wait_ge(normed, NT)
            nc.vector.tensor_tensor(xs[:, :, :], xs[:, :, :], over_tiles(b2_b), ALU.add).then_inc(prep, 1)

            dve.wait_ge(edges_in, 48)
            nc.vector.tensor_tensor(keep[:, 1:CH], dst_sb[:, 1:CH], dst_sb[:, 0:CH - 1],
                                    ALU.is_equal).then_inc(prep, 1)
            dve.wait_ge(ends_in, 64)
            nc.vector.tensor_copy(ends_f[:, :], ends[:, :]).then_inc(prep, 1)
            dve.wait_ge(prep, 2)
            nc.vector.tensor_scalar(keep[:, 1:CH], keep[:, 1:CH], 2.0, -1.0, ALU.mult, ALU.add).then_inc(prep, 1)
            dve.wait_ge(prep, 3)
            nc.vector.tensor_tensor(flag[:, 0:1], ends_f[:, 1:2], ends_f[:, 2:3], ALU.is_equal).then_inc(prep, 1)
            nc.vector.tensor_tensor(flag[:, 1:2], ends_f[:, 0:1], ends_f[:, 2:3], ALU.is_equal).then_inc(prep, 1)
            nc.vector.tensor_tensor(flag[:, 2:3], ends_f[:, 0:1], ends_f[:, 3:4], ALU.not_equal).then_inc(prep, 1)
            dve.wait_ge(prep, 4)
            nc.vector.tensor_scalar(keep[:, 1:CH], keep[:, 1:CH], LIMIT, None, ALU.mult).then_inc(prep, 1)
            dve.wait_ge(prep, 7)
            nc.vector.tensor_tensor(flag[:, 1:2], flag[:, 1:2], flag[:, 2:3], ALU.mult).then_inc(prep, 1)
            nc.vector.tensor_scalar(flag[:, 0:1], flag[:, 0:1], 2.0, -1.0, ALU.mult, ALU.add).then_inc(prep, 1)
            dve.wait_ge(prep, 9)
            nc.vector.scalar_tensor_tensor(out=flag[:, 3:4], in0=ends_f[:, 0:1], scalar=1.0, in1=flag[:, 1:2],
                                           op0=ALU.add, op1=ALU.mult).then_inc(prep, 1)
            dve.wait_ge(prep, 10)
            nc.vector.tensor_scalar(cmask[:, :], ones[:, 0:P], flag[:, 0:1], LIMIT, ALU.mult,
                                    ALU.mult).then_inc(cmask_made, 1)
            dve.wait_ge(prep, 11)
            nc.vector.tensor_scalar(key_t[:, :], minus_t[:, :], flag[:, 3:4], -1.0, ALU.add,
                                    ALU.add).then_inc(prep, 1)

            for b in range(NSB):
                dve.wait_ge(rows_in[b], 16 * SB_)
                with dve.Fori(0, SB_ // 2) as i:
                    for j in range(2):
                        c = i * 2 + (b * SB_ + j)
                        dve.wait_ge(counted, c + (NS + 2))
                        nc.vector.scalar_tensor_tensor(
                            out=junk[:, j, 0:ROW], in0=rows[:, bass.ds(c, 1), :].rearrange("p a r -> p (a r)"),
                            scalar=node_id[:, bass.ds(c, 1)], in1=ones[:, :], op0=ALU.is_le, op1=ALU.mult,
                            accum_out=cnt2[:, bass.ds(c, 1)]).then_inc(counted, 1)
            dve.wait_ge(counted, 2 * NS + 3)
            nc.vector.scalar_tensor_tensor(out=last_f[:, :], in0=row_f[:, :], scalar=float(ROW), in1=cnt2[:, :],
                                           op0=ALU.mult, op1=ALU.add).then_inc(prep, 1)
            dve.wait_ge(prep, 13)
            nc.vector.tensor_tensor(has[:, :], last_f[:, 1:NS], last_f[:, 0:NT], ALU.is_gt).then_inc(prep, 1)
            nc.vector.tensor_scalar(last_i[:, :], last_f[:, :], -1.0, 0.0, ALU.add, ALU.max).then_inc(last_made, 1)
            dve.wait_ge(p_taken, NTG)
            nc.vector.tensor_tensor(pm[:, :, :], pm[:, :, :], over_tiles(bm_b), ALU.add).then_inc(prep, 1)
            dve.wait_ge(prep, 15)
            nc.vector.tensor_tensor(pm[:, :, :], pm[:, :, :],
                                    has[:, :].rearrange("p (t a) -> p t a", a=1).broadcast_to([P, NT, D]),
                                    ALU.mult).then_inc(prep, 1)

            dve.wait_ge(h_kept[0], 16 * (NTG - NTG // 2))
            dve.wait_ge(h_kept[1], 16 * (NTG // 2))
            def edge_loop(i, first):
                for s in range(SLOTS):
                    base = i * (OPS * SLOTS) + OPS * s

                    def message(j):
                        nc.vector.scalar_tensor_tensor(
                            out=gath[:, s, j, :], in0=ww_b[:, :], scalar=w_sb[:, bass.ds(i * PER_LOOP + s * G + j, 1)],
                            in1=gath[:, s, j, :], op0=ALU.mult, op1=ALU.add).then_inc(edge_step, 1)

                    def maximum(j):
                        before = runm[:, s, j - 1, :] if j else runm[:, (s - 1) % SLOTS, G - 1, :]
                        dve.wait_ge(edge_step, base + (2 * j + 1))
                        nc.vector.scalar_tensor_tensor(
                            out=runm[:, s, j, :], in0=before, scalar=keep[:, bass.ds(i * PER_LOOP + s * G + j, 1)],
                            in1=gath[:, s, j, :], op0=ALU.min, op1=ALU.max).then_inc(edge_step, 1)

                    dve.wait_ge(gathered[s], 16 * G * (i + 1))
                    if not first:
                        dve.wait_ge(m_stored[s], 16 * i)
                    message(0)
                    for j in range(1, G):
                        message(j)
                        maximum(j - 1)
                    maximum(G - 1)

            edge_loop(0, True)
            with dve.Fori(1, LOOPS) as i:
                edge_loop(i, False)

            def onehots(g, n):
                for j in range(n):
                    nc.vector.tensor_scalar(onehot[:, j, :], tile_step[:, :], key_t[:, bass.ds(g * UG + j, 1)], None,
                                            ALU.is_equal).then_inc(onehot_made, 1)

            dve.wait_ge(cmask_spread, 1)
            nc.vector.tensor_copy(cmask_T[:, :], ps_cmask).then_inc(carry_step, 1)
            dve.wait_ge(carry_step, 1)
            dve.wait_ge(F_turned, 1)
            nc.vector.tensor_tensor_scan(ct[:, 1:P + 1], cmask_T[:, :], ps_F, 0.0, ALU.min,
                                         ALU.max).then_inc(carry_step, 1)
            dve.wait_ge(prep, 16)
            onehots(0, UG)
            dve.wait_ge(C_turned, 1)
            nc.vector.tensor_copy(cprev[:, :], ps_C).then_inc(carry_ready, 1)

            def finish_group(g, slot, n):
                dve.wait_ge(out_made, g + 1)
                nc.vector.tensor_tensor(xs[:, bass.ds(g * UG, n), :], ps_out[slot][:, 0:n, :],
                                        xs[:, bass.ds(g * UG, n), :], ALU.add).then_inc(res_made, 1)

            def update_group(g, i, slot, n, n_next, first):
                dve.wait_ge(fix_made, g + 1)
                for j in range(n):
                    dve.wait_ge(m_gathered[slot][j], 16 * (i + 1))
                    nc.vector.scalar_tensor_tensor(out=mmax[:, j, :], in0=ps_fix[:, j, :], scalar=ps_neg[:, j:j + 1],
                                                   in1=gath[:, slot, j, :], op0=ALU.add, op1=ALU.max
                                                   ).then_inc(joined, 1)
                if not first:
                    dve.wait_ge(aggT_made, g)
                for j in range(n):
                    t = g * UG + j
                    dve.wait_ge(joined, t + 1)
                    nc.vector.scalar_tensor_tensor(out=agg[:, slot, j, :], in0=mmax[:, j, :],
                                                   scalar=has[:, bass.ds(t, 1)],
                                                   in1=pm[:, bass.ds(t, 1), :].rearrange("p a f -> p (a f)"),
                                                   op0=ALU.mult, op1=ALU.add).then_inc(agg_made, 1)
                if n_next:
                    onehots(g + 1, n_next)
                if not first:
                    finish_group(g - 1, 1 - slot, UG)

            update_group(0, 0, 0, UG, UG, True)
            with dve.Fori(0, (NUG - 3) // 2) as i:
                update_group(2 * i + 1, i, 1, UG, UG, False)
                update_group(2 * i + 2, i + 1, 0, UG, UG, False)
            update_group(NUG - 2, (NUG - 3) // 2, 1, UG, LAST_UG, False)
            update_group(NUG - 1, (NUG - 1) // 2, 0, LAST_UG, 0, False)
            finish_group(NUG - 1, 0, LAST_UG)

        @block.tensor
        def _(pe):
            pe.wait_ge(counted, 1)
            pe.wait_ge(const_made, CONSTS)
            nc.tensor.matmul(ps_heads, ones[0:1, 0:P], head_f[:, :], start=True, stop=True).then_inc(heads_spread, 1)
            pe.wait_ge(weights_in, 16 * WEIGHTS)
            pe.wait_ge(counted, 2)

            def table_group(g, slot, first):
                for j in range(TG):
                    pe.wait_ge(normed, g * TG + j + 1)
                    last = nc.tensor.transpose(ps_xT[slot][:, j * P:(j + 1) * P], xn[:, slot, j, :], ident[:, :])
                last.then_inc(xT_made, 1)
                pe.wait_ge(h_made, g + 1)
                if not first:
                    pe.wait_ge(p_taken, g)
                for j in range(TG):
                    last = nc.tensor.matmul(ps_qp[:, j, :], hring[:, slot, j * P:(j + 1) * P], wsd[:, :],
                                            start=True, stop=True)
                last.then_inc(qp_made, 1)

            table_group(0, 0, True)
            table_group(1, 1, False)
            with pe.Fori(1, NTG // 2) as i:
                table_group(2 * i, 0, False)
                table_group(2 * i + 1, 1, False)
            table_group(NTG - 1, 0, False)

            pe.wait_ge(cmask_made, 1)
            nc.tensor.transpose(ps_cmask, cmask[:, :], ident[:, :]).then_inc(cmask_spread, 1)
            pe.wait_ge(edge_step, OPS * SLOTS * LOOPS)
            nc.tensor.transpose(ps_F, runm[:, SLOTS - 1, G - 1, :], ident[:, :]).then_inc(F_turned, 1)
            pe.wait_ge(carry_step, 2)
            nc.tensor.transpose(ps_C, ct[:, 0:P], ident[:, :]).then_inc(C_turned, 1)
            pe.wait_ge(carry_ready, 1)

            def carries(g, n, first=False):
                pe.wait_ge(onehot_made, g * UG + n)
                if not first:
                    pe.wait_ge(joined, g * UG)
                for j in range(n):
                    nc.tensor.matmul(ps_fix[:, j, :], onehot[:, j, :], cprev[:, :], start=True, stop=True)
                    nc.tensor.matmul(ps_neg[:, j:j + 1], onehot[:, j, :], huge_col[:, :], start=True, stop=False)
                    last = nc.tensor.matmul(ps_neg[:, j:j + 1], ones[0:1, 0:P], minus_huge[:, :],
                                            start=False, stop=True)
                last.then_inc(fix_made, 1)

            def update_group(g, slot, n, n_next, wait):
                pe.wait_ge(agg_made, g * UG + n)
                if wait:
                    pe.wait_ge(aggT_kept, g - 1)
                for j in range(n):
                    last = nc.tensor.transpose(ps_aggT[slot][:, j * P:(j + 1) * P], agg[:, slot, j, :], ident[:, :])
                last.then_inc(aggT_made, 1)
                if wait:
                    pe.wait_ge(hid_kept, g - 1)
                nc.tensor.matmul(ps_hid[slot][:, 0:n * P], w1a[:, :], hT[:, bass.ds(g * (UG * P), n * P)],
                                 start=True, stop=False)
                pe.wait_ge(aggT_kept, g + 1)
                nc.tensor.matmul(ps_hid[slot][:, 0:n * P], w1b[:, :], aggT[:, slot, 0:n * P],
                                 start=False, stop=True).then_inc(hid_made, 1)
                if n_next:
                    carries(g + 1, n_next)
                pe.wait_ge(hid_kept, g + 1)
                if wait:
                    pe.wait_ge(res_made, g - 1)
                for j in range(n):
                    last = nc.tensor.matmul(ps_out[slot][:, j, :], hidT[:, slot, j * P:(j + 1) * P], w2[:, :],
                                            start=True, stop=True)
                last.then_inc(out_made, 1)

            carries(0, UG, True)
            pe.wait_ge(h_kept[0], 16 * (NTG - NTG // 2))
            pe.wait_ge(h_kept[1], 16 * (NTG // 2))
            update_group(0, 0, UG, UG, False)
            update_group(1, 1, UG, UG, False)
            with pe.Fori(1, NUG // 2 - 1) as i:
                update_group(2 * i, 0, UG, UG, True)
                update_group(2 * i + 1, 1, UG, UG, True)
            update_group(NUG - 3, 0, UG, UG, True)
            update_group(NUG - 2, 1, UG, LAST_UG, True)
            update_group(NUG - 1, 0, LAST_UG, 0, True)


_INS = ['x', 'src', 'dst', 'edge_weight', 'L0_gnn_Wm', 'L0_gnn_bm', 'L0_gnn_W1', 'L0_gnn_b1', 'L0_gnn_W2', 'L0_gnn_b2']


def kernel(**inputs):
    import numpy as _np
    import concourse.bacc as _bacc
    from concourse import mybir as _mybir
    from concourse.bass_utils import run_bass_kernel_spmd as _run

    nc = _bacc.Bacc("TRN2", target_bir_lowering=False, num_devices=1)
    pads = {'x': (NN, 0), 'src': (NE, 0), 'dst': (NE, N_NODES), 'edge_weight': (NE, 0)}
    arrays, args = {}, []
    for name in _INS:
        a = _np.ascontiguousarray(inputs[name])
        if name in pads:
            n, value = pads[name]
            padded = _np.full((n,) + a.shape[1:], value, a.dtype)
            padded[:len(a)] = a
            a = padded
        arrays[f"in_{name}_dram"] = a
        args.append(nc.dram_tensor(f"in_{name}_dram", a.shape, _mybir.dt.from_np(a.dtype), kind="ExternalInput").ap())
    q_tab = nc.dram_tensor("q_tab", (NN, D), _mybir.dt.float32, kind="Internal").ap()
    m_tab = nc.dram_tensor("m_tab", (NE, D), _mybir.dt.float32, kind="Internal").ap()
    out = nc.dram_tensor("out_0_dram", (NN, D), _mybir.dt.float32, kind="ExternalOutput").ap()
    build(nc, *args, q_tab, m_tab, out)
    r = _run(nc, [arrays], core_ids=[0])
    return r.results[0]["out_0_dram"][:N_NODES]
```

```python
from contextlib import ExitStack

import concourse.bass as bass
from concourse import mybir

F32 = mybir.dt.float32
I32 = mybir.dt.int32
BF16 = mybir.dt.bfloat16
ALU = mybir.AluOpType
ACT = mybir.ActivationFunctionType

P = 128
D = 128
N_NODES = 6250
N_EDGES = 106250
NT = -(-N_NODES // P)
NN = P * NT
G = 4
SLOTS = 8
PER_LOOP = G * SLOTS
CH = -(-N_EDGES // (P * PER_LOOP)) * PER_LOOP
NE = P * CH
LOOPS = CH // PER_LOOP
HALF = SLOTS // 2
LOOPS_A = LOOPS * 3 // 4
NS = NT + 1
H = 8
NH = CH // H
ROUND = 1.5 * 2.0 ** 23
TG = 7
NTG = NT // TG
UG = 4
NUG = -(-NT // UG)
LAST_UG = NT - (NUG - 1) * UG
LIMIT = 3.4028234663852886e38
HUGE = 2.0 ** 127
EPS = 1e-5
OPS = 2 * G
assert PER_LOOP > 4 * TG and UG <= G and NT % TG == 0 and NT % 2 == 1 and NH % 2 == 0 and NTG % 2 == 1 and NUG % 2 == 1


def build(nc, x, src, dst, ew, Wm, bm, W1, b1, W2, b2, q_tab, m_tab, out):
    ctx = ExitStack()
    with ctx:
        def sb(name, shape, dt=F32):
            return ctx.enter_context(nc.sbuf_tensor(name, shape, dt))

        def sem(name):
            return ctx.enter_context(nc.semaphore(name))

        xs = sb("xs", [P, NT, D])
        hT = sb("hT", [P, NT * P])
        pm = sb("pm", [P, NT, D])
        dst_sb = sb("dst_sb", [P, CH], I32)
        minus_a = sb("minus_a", [P, CH])
        minus_b = sb("minus_b", [P, CH])
        dst_f = sb("dst_f", [P, CH])
        w_sb = sb("w_sb", [P, CH])
        keep = sb("keep", [P, CH])
        gath = sb("gath", [P, SLOTS, G, D])
        runm = sb("runm", [P, SLOTS, G, D])
        ring_a = gath[:, :, :, :].rearrange("p s j f -> p (s j) f")
        ring_b = runm[:, :, :, :].rearrange("p s j f -> p (s j) f")
        xn = ring_a[:, 0:2 * TG, :].rearrange("p (s t) f -> p s t f", s=2)
        hring = ring_b[:, 0:2 * TG, :].rearrange("p (s t) f -> p s (t f)", s=2)
        q_sb = ring_b[:, 2 * TG:4 * TG, :].rearrange("p (s t) f -> p s t f", s=2)
        ident = sb("ident", [P, P])
        ws = sb("ws", [P, D])
        wd = sb("wd", [P, D])
        w1a = sb("w1a", [P, D])
        w1b = sb("w1b", [P, D])
        w2 = sb("w2", [P, D])
        ww_b = sb("ww_b", [P, D])
        b2_b = sb("b2_b", [P, D])
        bm_row = sb("bm_row", [1, D])
        h_fix = sb("h_fix", [P, TG * P])
        b1_col = sb("b1_col", [P, 1])
        ones = sb("ones", [P, P])
        a_row = sb("a_row", [P, P + 1])
        b_row = sb("b_row", [P, NS])
        a_sign = sb("a_sign", [P, 2, H, P + 2], BF16)
        b_sign = sb("b_sign", [P, 2, H, NS], BF16)
        count_a = sb("count_a", [P, NS])
        count_b = sb("count_b", [P, NS])
        count_0 = sb("count_0", [P, 1])
        tile_step = sb("tile_step", [P, P])
        minus_t = sb("minus_t", [P, NT])
        src_idx = sb("src_idx", [P, 2, PER_LOOP // 2], I32)
        last_idx = sb("last_idx", [P, 2, UG], I32)
        last_f = sb("last_f", [P, NS])
        last_i = sb("last_i", [P, NS], I32)
        has = sb("has", [P, NT])
        stats = sb("stats", [P, NT, 6])
        mean = sb("mean", [P, NT])
        diff = sb("diff", [P, NT])
        var = sb("var", [P, NT])
        std = sb("std", [P, NT])
        rstd = sb("rstd", [P, NT])
        shift = sb("shift", [P, NT])
        eps_col = sb("eps_col", [P, 1])
        ends = sb("ends", [P, 4], I32)
        ends_f = sb("ends_f", [P, 4])
        flag = sb("flag", [P, 4])
        split_key = sb("split_key", [P, 3])
        key_t = sb("key_t", [P, NT])
        cmask = sb("cmask", [P, P])
        cmask_T = sb("cmask_T", [P, P])
        ct = sb("ct", [P, P + 1])
        cprev = sb("cprev", [P, D])
        drop = sb("drop", [P, NT])
        sel_p = sb("sel_p", [P, P])
        sel_t = sb("sel_t", [P, NT])
        onehot = sb("onehot", [P, 2, UG, P])
        mmax = sb("mmax", [P, 2, UG, D])
        agg = sb("agg", [P, 2, UG, D])
        aggT = sb("aggT", [P, 2, UG * P])
        hidT = sb("hidT", [P, 2, UG * P])

        ps = ctx.enter_context(nc.psum_tensor("ps", [P, 8, 512], F32))
        ps_xT = [ps[:, 2 * i:2 * i + 2, :].rearrange("p b c -> p (b c)") for i in range(2)]
        ps_q = [ps[:, 4 + 2 * i:6 + 2 * i, :].rearrange("p b c -> p (b c)") for i in range(2)]
        ps_p = ps[:, 0:2, :].rearrange("p b c -> p (b c)")
        ps_count = [ps[:, 2 + i, 0:NS] for i in range(2)]
        ps_cmask = ps[:, 4, 0:P]
        ps_F = ps[:, 5, 0:P]
        ps_C = ps[:, 6, 0:P]
        ps_fix = ps[:, 0, :].rearrange("p (j f) -> p j f", f=D)
        ps_sel = ps[:, 7, 0:NT]
        ps_aggT = [ps[:, 2 + i, :] for i in range(2)]
        ps_hid = [ps[:, 4 + i, :] for i in range(2)]
        ps_out = [ps[:, 6 + i, :].rearrange("p (j f) -> p j f", f=D) for i in range(2)]

        const_made = sem("const_made")
        ident_zero = sem("ident_zero")
        rows_made = sem("rows_made")
        ends_clear = sem("ends_clear")
        x_in = [sem(f"x_in{g}") for g in range(NTG)]
        weights_in = sem("weights_in")
        ws_in = sem("ws_in")
        ww_in = sem("ww_in")
        edges_in = sem("edges_in")
        ends_in = sem("ends_in")
        split_made = sem("split_made")
        signs_made = sem("signs_made")
        signs_used = sem("signs_used")
        h_fixed = sem("h_fixed")
        p_made = sem("p_made")
        p_taken = sem("p_taken")
        src_idx_in = [sem(f"src_idx_in{i}") for i in range(2)]
        last_idx_made = sem("last_idx_made")
        std_made = sem("std_made")
        normed = sem("normed")
        xT_made = sem("xT_made")
        h_made = sem("h_made")
        h_kept = [sem(f"h_kept{i}") for i in range(2)]
        q_made = sem("q_made")
        q_taken = sem("q_taken")
        q_stored = [sem(f"q_stored{i}") for i in range(2)]
        edge_step = sem("edge_step")
        gathered = [sem(f"gathered{i}") for i in range(SLOTS)]
        m_stored = [sem(f"m_stored{i}") for i in range(SLOTS)]
        cmask_spread = sem("cmask_spread")
        F_turned = sem("F_turned")
        carry_step = sem("carry_step")
        C_turned = sem("C_turned")
        carry_ready = sem("carry_ready")
        onehot_made = sem("onehot_made")
        fix_made = sem("fix_made")
        m_gathered = [[sem(f"m_gathered{s}_{j}") for j in range(UG)] for s in range(2)]
        joined = sem("joined")
        agg_made = sem("agg_made")
        aggT_made = sem("aggT_made")
        aggT_kept = sem("aggT_kept")
        hid_made = sem("hid_made")
        hid_kept = sem("hid_kept")
        out_made = sem("out_made")
        res_made = sem("res_made")
        res_stored = sem("res_stored")
        block = ctx.enter_context(nc.Block())

        stat_step = sem("stat_step")
        var_made = sem("var_made")
        rstd_made = sem("rstd_made")
        shift_made = sem("shift_made")
        prep = sem("prep")
        count_step = sem("count_step")
        cmask_made = sem("cmask_made")
        key_step = sem("key_step")
        sel_made = sem("sel_made")
        sel_summed = sem("sel_summed")
        last_made = sem("last_made")
        m_rows = m_tab.rearrange("(p j) f -> p j f", p=P)
        q_rows = q_tab.rearrange("(p t) f -> p t f", p=P)
        out_rows = out.rearrange("(p t) f -> p t f", p=P)
        CONSTS = 10
        WEIGHTS = 7
        x_tiles = x.rearrange("(p t) f -> p t f", p=P)
        src_pj = src.rearrange("(p j) -> p j", p=P)
        dst_pj = dst.rearrange("(p j) -> p j", p=P)

        @block.sync
        def _(sp):
            for g in range(NTG):
                sp.dma_start(xs[:, g * TG:(g + 1) * TG, :], x_tiles[:, g * TG:(g + 1) * TG, :]).then_inc(x_in[g], 16)

            def load_indices(i, half):
                sp.dma_start(src_idx[:, half, :],
                             src_pj[:, bass.ds(i * PER_LOOP + half * (PER_LOOP // 2), PER_LOOP // 2)]
                             ).then_inc(src_idx_in[half], 16)

            load_indices(0, 0)
            load_indices(0, 1)
            sp.dma_start(dst_sb[:, :], dst_pj).then_inc(edges_in, 16)
            sp.dma_start(w_sb[:, :], ew.rearrange("(p j) -> p j", p=P)).then_inc(edges_in, 16)

            def table_group(g, slot):
                sp.wait_ge(h_made, g + 1)
                sp.dma_start(hT[:, bass.ds(g * (TG * P), TG * P)], hring[:, slot, :]).then_inc(h_kept[slot], 16)
                sp.wait_ge(q_taken, g + 1)
                sp.dma_start(q_rows[:, bass.ds(g * TG, TG), :], q_sb[:, slot, :, :]).then_inc(q_stored[slot], 16)

            with sp.Fori(0, NTG // 2) as i:
                table_group(2 * i, 0)
                table_group(2 * i + 1, 1)
            table_group(NTG - 1, 0)

            def edge_loop(i, last):
                for s in range(SLOTS):
                    sp.wait_ge(edge_step, i * (OPS * SLOTS) + OPS * (s + 1))
                    sp.dma_start(m_rows[:, bass.ds(i * PER_LOOP + s * G, G), :],
                                 runm[:, s, :, :]).then_inc(m_stored[s], 16)
                    if s % HALF == HALF - 1 and not last:
                        load_indices(i + 1, s // HALF)

            with sp.Fori(0, LOOPS - 1) as i:
                edge_loop(i, False)
            edge_loop(LOOPS - 1, True)

            def update_group(g, n):
                sp.wait_ge(res_made, g + 1)
                sp.dma_start(out_rows[:, bass.ds(g * UG, n), :],
                             xs[:, bass.ds(g * UG, n), :]).then_inc(res_stored, 16)

            with sp.Fori(0, NUG - 1) as g:
                update_group(g, UG)
            update_group(NUG - 1, LAST_UG)
            sp.wait_ge(res_stored, 16 * NUG)

        @block.gpsimd
        def _(pool):
            pool.memset(ones[:, :], 1.0).then_inc(const_made, 1)
            pool.memset(ends[:, :], -1).then_inc(ends_clear, 1)
            pool.iota(a_row[:, :], [[1, P + 1]], base=0, channel_multiplier=0,
                      allow_small_or_imprecise_dtypes=True).then_inc(rows_made, 1)
            pool.iota(b_row[:, :], [[1, NS]], base=0, channel_multiplier=0,
                      allow_small_or_imprecise_dtypes=True).then_inc(rows_made, 1)
            pool.wait_ge(rows_made, 2)
            pool.tensor_scalar(a_row[:, :], a_row[:, :], -0.5, 1.0, ALU.add, ALU.mult).then_inc(const_made, 1)
            pool.tensor_scalar(b_row[:, :], b_row[:, :], -0.5, 1.0, ALU.add, ALU.mult).then_inc(const_made, 1)
            pool.memset(eps_col[:, :], EPS).then_inc(const_made, 1)
            pool.memset(ident[:, :], 0.0).then_inc(ident_zero, 1)
            pool.wait_ge(ident_zero, 1)
            pool.affine_select(out=ident[:, :], in_=ident[:, :], compare_op=ALU.not_equal, fill=1.0, base=0,
                               pattern=[[-1, P]], channel_multiplier=1).then_inc(const_made, 1)
            pool.iota(tile_step[:, :], [[NT, P]], base=0, channel_multiplier=0,
                      allow_small_or_imprecise_dtypes=True).then_inc(const_made, 1)
            pool.iota(minus_t[:, :], [[-1, NT]], base=0, channel_multiplier=0,
                      allow_small_or_imprecise_dtypes=True).then_inc(const_made, 1)
            pool.memset(keep[:, 0:1], -LIMIT).then_inc(const_made, 1)
            pool.memset(runm[:, SLOTS - 1, G - 1, :], 0.0).then_inc(const_made, 1)
            pool.memset(ct[:, 0:1], 0.0).then_inc(const_made, 1)

            for g in range(NTG):
                pool.wait_ge(shift_made, g + 1)
                if g >= 2:
                    pool.wait_ge(xT_made, g - 1)
                for t in range(g * TG, (g + 1) * TG):
                    pool.tensor_scalar(xn[:, g % 2, t % TG, :], xs[:, t, :], rstd[:, t:t + 1], shift[:, t:t + 1],
                                       ALU.mult, ALU.add).then_inc(normed, 1)

            pool.wait_ge(q_stored[0], 16 * (NTG - NTG // 2))
            pool.wait_ge(q_stored[1], 16 * (NTG // 2))

            def gather_group(i, s):
                pool.wait_ge(src_idx_in[s // HALF], 16 * (i + 1))
                pool.nop(nofuse=True)
                for j in range(G):
                    pool.indirect_dma_start(gath[:, s, j, :], None, q_tab,
                                            bass.IndirectOffsetOnAxis(
                                                src_idx[:, s // HALF, s % HALF * G + j:s % HALF * G + j + 1], 0)
                                            ).then_inc(gathered[s], 16)

            for s in range(SLOTS):
                gather_group(0, s)
            with pool.Fori(1, LOOPS) as i:
                for s in range(SLOTS):
                    pool.wait_ge(edge_step, (i - 1) * (OPS * SLOTS) + OPS * (s + 1))
                    pool.nop(nofuse=True)
                    gather_group(i, s)

            for s in range(SLOTS):
                pool.wait_ge(m_stored[s], 16 * LOOPS)
            pool.wait_ge(last_made, 1)
            pool.wait_ge(edge_step, OPS * SLOTS * LOOPS)

            def update_group(g, slot, n, wait):
                if wait:
                    pool.wait_ge(joined, (g - 1) * UG)
                pool.tensor_copy(last_idx[:, slot, 0:n], last_i[:, bass.ds(g * UG + 1, n)]).then_inc(last_idx_made, 1)
                pool.wait_ge(last_idx_made, g + 1)
                pool.nop(nofuse=True)
                for j in range(n):
                    pool.indirect_dma_start(gath[:, slot, j, :], None, m_tab,
                                            bass.IndirectOffsetOnAxis(last_idx[:, slot, j:j + 1], 0)
                                            ).then_inc(m_gathered[slot][j], 16)

            update_group(0, 0, UG, False)
            update_group(1, 1, UG, False)
            with pool.Fori(1, NUG // 2) as i:
                update_group(2 * i, 0, UG, True)
                update_group(2 * i + 1, 1, UG, True)
            update_group(NUG - 1, 0, LAST_UG, True)

        @block.scalar
        def _(act):
            act.dma_start(ws[:, :], Wm[D:2 * D, :]).then_inc(ws_in, 16)
            act.dma_start(ww_b[:, :], Wm[2 * D:2 * D + 1, :].broadcast_to([P, D])).then_inc(ww_in, 16)

            act.wait_ge(const_made, CONSTS)

            def std_group(g):
                act.wait_ge(var_made, g + 1)
                nc.scalar.activation(std[:, bass.ds(g * TG, TG)], var[:, bass.ds(g * TG, TG)], ACT.Sqrt,
                                     bias=eps_col[:, 0:1]).then_inc(std_made, 1)

            def take_group(i, slot, first):
                g = 2 * i + slot
                act.wait_ge(xT_made, g + 1)
                if not first:
                    act.wait_ge(h_kept[slot], 16 * i)
                    act.wait_ge(q_made, g - 1)
                nc.scalar.activation(hring[:, slot, :], ps_xT[slot][:, 0:TG * P], ACT.Relu).then_inc(h_made, 1)
                act.wait_ge(q_made, g + 1)
                if not first:
                    act.wait_ge(q_stored[slot], 16 * i)
                nc.scalar.copy(q_sb[:, slot, :, :], ps_q[slot][:, 0:TG * D].rearrange("p (t f) -> p t f", f=D)
                               ).then_inc(q_taken, 1)

            std_group(0)
            std_group(1)
            take_group(0, 0, True)
            std_group(2)
            take_group(0, 1, True)
            with act.Fori(1, NTG // 2) as i:
                std_group(2 * i + 1)
                take_group(i, 0, False)
                std_group(2 * i + 2)
                take_group(i, 1, False)
            take_group(NTG // 2, 0, False)

            with nc.allow_non_contiguous_dma(reason="one entry for each partition"):
                act.dma_start(ends[:, 0:1], dst_pj[:, 0:1]).then_inc(ends_in, 16)
                act.dma_start(ends[:, 1:2], dst_pj[:, CH - 1:CH]).then_inc(ends_in, 16)
                act.dma_start(ends[1:P, 2:3], dst_pj[0:P - 1, CH - 1:CH]).then_inc(ends_in, 16)
                act.dma_start(ends[0:P - 1, 3:4], dst_pj[1:P, 0:1]).then_inc(ends_in, 16)
                act.dma_start(b1_col[:, :], b1.rearrange("(f a) -> f a", a=1)).then_inc(weights_in, 16)
            act.dma_start(wd[:, :], Wm[0:D, :]).then_inc(weights_in, 16)
            act.dma_start(bm_row[:, :], bm.rearrange("(a f) -> a f", a=1)).then_inc(weights_in, 16)
            act.dma_start(b2_b[:, :], b2.rearrange("(a f) -> a f", a=1).broadcast_to([P, D])).then_inc(weights_in, 16)
            act.dma_start(w1a[:, :], W1[0:D, :]).then_inc(weights_in, 16)
            act.dma_start(w1b[:, :], W1[D:2 * D, :]).then_inc(weights_in, 16)
            act.dma_start(w2[:, :], W2).then_inc(weights_in, 16)

            act.wait_ge(h_kept[0], 16 * (NTG - NTG // 2))
            act.wait_ge(h_kept[1], 16 * (NTG // 2))
            with act.Fori(0, NTG) as g:
                nc.scalar.copy(h_fix[:, :], hT[:, bass.ds(g * (TG * P), TG * P)]).then_inc(h_fixed, 1)
                act.wait_ge(p_made, g + 1)
                nc.scalar.copy(pm[:, bass.ds(g * TG, TG), :],
                               ps_p[:, 0:TG * D].rearrange("p (t f) -> p t f", f=D)).then_inc(p_taken, 1)

            act.wait_ge(split_made, 2)

            def signs(i, slot, first):
                if not first:
                    act.wait_ge(signs_used, 2 * i + slot - 1)
                for j in range(H):
                    k = (2 * i + slot) * H + j
                    nc.scalar.activation(a_sign[:, slot, j, 0:P + 1], a_row[:, :], ACT.Sign,
                                         bias=minus_a[:, bass.ds(k, 1)])
                    nc.scalar.activation(b_sign[:, slot, j, :], b_row[:, :], ACT.Sign,
                                         bias=minus_b[:, bass.ds(k, 1)]).then_inc(signs_made, 1)

            signs(0, 0, True)
            signs(0, 1, True)
            with act.Fori(1, NH // 2) as i:
                signs(i, 0, False)
                signs(i, 1, False)

            def update_group(g, slot, n, wait):
                act.wait_ge(aggT_made, g + 1)
                if wait:
                    act.wait_ge(hid_made, g - 1)
                nc.scalar.copy(aggT[:, slot, 0:n * P], ps_aggT[slot][:, 0:n * P]).then_inc(aggT_kept, 1)
                act.wait_ge(hid_made, g + 1)
                if wait:
                    act.wait_ge(out_made, g - 1)
                nc.scalar.activation(hidT[:, slot, 0:n * P], ps_hid[slot][:, 0:n * P], ACT.Relu,
                                     bias=b1_col[:, 0:1]).then_inc(hid_kept, 1)

            update_group(0, 0, UG, False)
            update_group(1, 1, UG, False)
            with act.Fori(1, NUG // 2) as i:
                update_group(2 * i, 0, UG, True)
                update_group(2 * i + 1, 1, UG, True)
            update_group(NUG - 1, 0, LAST_UG, True)

        @block.vector
        def _(dve):
            def stats_group(g, arrived):
                dve.wait_ge(arrived, 16)
                for j in range(TG):
                    nc.vector.bn_stats(stats[:, g * TG + j, :], xs[:, g * TG + j, :]).then_inc(stat_step, 1)
                tiles = slice(g * TG, (g + 1) * TG)
                done = g * (TG + 5)
                dve.wait_ge(stat_step, done + TG)
                nc.vector.tensor_tensor(mean[:, tiles], stats[:, tiles, 1], stats[:, tiles, 4],
                                        ALU.add).then_inc(stat_step, 1)
                nc.vector.tensor_tensor(diff[:, tiles], stats[:, tiles, 1], stats[:, tiles, 4],
                                        ALU.subtract).then_inc(stat_step, 1)
                nc.vector.tensor_tensor(var[:, tiles], stats[:, tiles, 2], stats[:, tiles, 5],
                                        ALU.add).then_inc(stat_step, 1)
                dve.wait_ge(stat_step, done + TG + 2)
                nc.vector.scalar_tensor_tensor(out=diff[:, tiles], in0=diff[:, tiles], scalar=0.25,
                                               in1=diff[:, tiles], op0=ALU.mult, op1=ALU.mult
                                               ).then_inc(stat_step, 1)
                nc.vector.tensor_scalar(mean[:, tiles], mean[:, tiles], 0.5, None, ALU.mult).then_inc(stat_step, 1)
                dve.wait_ge(stat_step, done + TG + 4)
                nc.vector.scalar_tensor_tensor(out=var[:, tiles], in0=var[:, tiles], scalar=1.0 / D,
                                               in1=diff[:, tiles], op0=ALU.mult, op1=ALU.add).then_inc(var_made, 1)

            def rstd_group(g):
                tiles = slice(g * TG, (g + 1) * TG)
                dve.wait_ge(std_made, g + 1)
                nc.vector.reciprocal(rstd[:, tiles], std[:, tiles]).then_inc(rstd_made, 1)
                dve.wait_ge(rstd_made, g + 1)
                nc.vector.scalar_tensor_tensor(out=shift[:, tiles], in0=mean[:, tiles], scalar=-1.0,
                                               in1=rstd[:, tiles], op0=ALU.mult, op1=ALU.mult
                                               ).then_inc(shift_made, 1)

            stats_group(0, x_in[0])
            for g in range(NTG):
                if g + 1 < NTG:
                    stats_group(g + 1, x_in[g + 1])
                rstd_group(g)

            dve.wait_ge(const_made, CONSTS)
            dve.wait_ge(weights_in, 16 * WEIGHTS)
            dve.wait_ge(normed, NT)
            nc.vector.tensor_tensor(xs[:, :, :], xs[:, :, :], b2_b[:, :].rearrange("p (t f) -> p t f", t=1).broadcast_to([P, NT, D]), ALU.add).then_inc(prep, 1)

            dve.wait_ge(edges_in, 32)
            nc.vector.tensor_tensor(keep[:, 1:CH], dst_sb[:, 1:CH], dst_sb[:, 0:CH - 1],
                                    ALU.is_equal).then_inc(prep, 1)
            dve.wait_ge(ends_in, 64)
            nc.vector.tensor_copy(ends_f[:, :], ends[:, :]).then_inc(prep, 1)
            dve.wait_ge(prep, 2)
            nc.vector.tensor_scalar(keep[:, 1:CH], keep[:, 1:CH], 2.0, -1.0, ALU.mult, ALU.add).then_inc(prep, 1)
            dve.wait_ge(prep, 3)
            nc.vector.tensor_tensor(flag[:, 0:1], ends_f[:, 1:2], ends_f[:, 2:3], ALU.is_equal).then_inc(prep, 1)
            nc.vector.tensor_tensor(flag[:, 1:2], ends_f[:, 0:1], ends_f[:, 2:3], ALU.is_equal).then_inc(prep, 1)
            nc.vector.tensor_tensor(flag[:, 2:3], ends_f[:, 0:1], ends_f[:, 3:4], ALU.not_equal).then_inc(prep, 1)
            dve.wait_ge(prep, 4)
            nc.vector.tensor_scalar(keep[:, 1:CH], keep[:, 1:CH], LIMIT, None, ALU.mult).then_inc(prep, 1)
            dve.wait_ge(prep, 7)
            nc.vector.tensor_tensor(flag[:, 1:2], flag[:, 1:2], flag[:, 2:3], ALU.mult).then_inc(prep, 1)
            nc.vector.tensor_scalar(flag[:, 0:1], flag[:, 0:1], 2.0, -1.0, ALU.mult, ALU.add).then_inc(prep, 1)
            dve.wait_ge(prep, 9)
            nc.vector.scalar_tensor_tensor(out=flag[:, 3:4], in0=ends_f[:, 0:1], scalar=1.0, in1=flag[:, 1:2],
                                           op0=ALU.add, op1=ALU.mult).then_inc(prep, 1)
            dve.wait_ge(prep, 10)
            nc.vector.tensor_scalar(cmask[:, :], ones[:, 0:P], flag[:, 0:1], LIMIT, ALU.mult,
                                    ALU.mult).then_inc(cmask_made, 1)
            dve.wait_ge(prep, 11)
            nc.vector.tensor_scalar(key_t[:, :], minus_t[:, :], flag[:, 3:4], -1.0, ALU.add,
                                    ALU.add).then_inc(prep, 1)

            nc.vector.tensor_scalar(split_key[:, 0:1], flag[:, 3:4], -1.0 - (NT - 1) / 2.0, 1.0 / NT, ALU.add,
                                    ALU.mult).then_inc(key_step, 1)
            dve.wait_ge(key_step, 1)
            nc.vector.tensor_scalar(split_key[:, 1:2], split_key[:, 0:1], ROUND, None, ALU.add).then_inc(key_step, 1)
            dve.wait_ge(key_step, 2)
            nc.vector.tensor_scalar(split_key[:, 2:3], split_key[:, 1:2], -ROUND, float(NT), ALU.add,
                                    ALU.mult).then_inc(key_step, 1)
            dve.wait_ge(key_step, 3)
            nc.vector.tensor_scalar(sel_p[:, :], tile_step[:, :], split_key[:, 2:3], None,
                                    ALU.is_equal).then_inc(sel_made, 1)
            dve.wait_ge(prep, 12)
            nc.vector.tensor_scalar(sel_t[:, :], key_t[:, :], split_key[:, 2:3], None,
                                    ALU.is_equal).then_inc(sel_made, 1)

            nc.vector.tensor_copy(dst_f[:, :], dst_sb[:, :]).then_inc(prep, 1)
            dve.wait_ge(prep, 13)
            nc.vector.tensor_scalar(minus_a[:, :], dst_f[:, :], -(NT - 1) / 2.0, 1.0 / NT, ALU.add,
                                    ALU.mult).then_inc(prep, 1)
            dve.wait_ge(prep, 14)
            nc.vector.tensor_scalar(minus_a[:, :], minus_a[:, :], ROUND, None, ALU.add).then_inc(prep, 1)
            dve.wait_ge(prep, 15)
            nc.vector.tensor_scalar(minus_a[:, :], minus_a[:, :], -ROUND, -1.0, ALU.add,
                                    ALU.mult).then_inc(split_made, 1)
            dve.wait_ge(split_made, 1)
            nc.vector.scalar_tensor_tensor(out=minus_b[:, :], in0=minus_a[:, :], scalar=float(NT), in1=dst_f[:, :],
                                           op0=ALU.mult, op1=ALU.add).then_inc(prep, 1)
            dve.wait_ge(prep, 16)
            nc.vector.tensor_scalar(minus_b[:, :], minus_b[:, :], -1.0, None, ALU.mult).then_inc(split_made, 1)

            dve.wait_ge(ww_in, 16)
            dve.wait_ge(h_kept[0], 16 * (NTG - NTG // 2))
            dve.wait_ge(h_kept[1], 16 * (NTG // 2))
            def edge_loop(i, first):
                for s in range(SLOTS):
                    base = i * (OPS * SLOTS) + OPS * s

                    def message(j):
                        nc.vector.scalar_tensor_tensor(
                            out=gath[:, s, j, :], in0=ww_b[:, :], scalar=w_sb[:, bass.ds(i * PER_LOOP + s * G + j, 1)],
                            in1=gath[:, s, j, :], op0=ALU.mult, op1=ALU.add).then_inc(edge_step, 1)

                    def maximum(j):
                        before = runm[:, s, j - 1, :] if j else runm[:, (s - 1) % SLOTS, G - 1, :]
                        dve.wait_ge(edge_step, base + (2 * j + 1))
                        nc.vector.scalar_tensor_tensor(
                            out=runm[:, s, j, :], in0=before, scalar=keep[:, bass.ds(i * PER_LOOP + s * G + j, 1)],
                            in1=gath[:, s, j, :], op0=ALU.min, op1=ALU.max).then_inc(edge_step, 1)

                    dve.wait_ge(gathered[s], 16 * G * (i + 1))
                    if not first:
                        dve.wait_ge(m_stored[s], 16 * i)
                    message(0)
                    for j in range(1, G):
                        message(j)
                        maximum(j - 1)
                    maximum(G - 1)

            edge_loop(0, True)
            with dve.Fori(1, LOOPS_A) as i:
                edge_loop(i, False)

            dve.wait_ge(signs_used, NH)
            nc.vector.tensor_copy(count_a[:, :], ps_count[0]).then_inc(count_step, 1)
            dve.wait_ge(count_step, 1)
            nc.vector.tensor_tensor(count_b[:, :], count_a[:, :], ps_count[1], ALU.subtract).then_inc(count_step, 1)
            nc.vector.tensor_tensor(count_0[:, :], count_a[:, 0:1], ps_count[1][:, 0:1],
                                    ALU.add).then_inc(count_step, 1)
            dve.wait_ge(count_step, 3)
            nc.vector.tensor_scalar(last_f[:, :], count_b[:, :], count_0[:, 0:1], 0.25, ALU.subtract,
                                    ALU.mult).then_inc(count_step, 1)
            dve.wait_ge(count_step, 4)
            nc.vector.tensor_scalar(last_f[:, :], last_f[:, :], NE / 2.0 - 1.0, None, ALU.add).then_inc(count_step, 1)
            dve.wait_ge(count_step, 5)
            nc.vector.tensor_scalar(last_i[:, :], last_f[:, :], 0.0, None, ALU.max).then_inc(last_made, 1)
            nc.vector.tensor_tensor(has[:, :], last_f[:, 1:NS], last_f[:, 0:NT], ALU.is_gt).then_inc(count_step, 1)
            dve.wait_ge(count_step, 6)
            dve.wait_ge(p_taken, NTG)
            nc.vector.tensor_tensor(pm[:, :, :], pm[:, :, :],
                                    has[:, :].rearrange("p (t a) -> p t a", a=1).broadcast_to([P, NT, D]),
                                    ALU.mult).then_inc(count_step, 1)
            dve.wait_ge(sel_summed, 1)
            nc.vector.tensor_scalar(drop[:, :], ps_sel, -1.0, HUGE, ALU.add, ALU.mult).then_inc(count_step, 1)

            with dve.Fori(LOOPS_A, LOOPS) as i:
                edge_loop(i, False)

            def onehots(g, slot, n):
                for j in range(n):
                    nc.vector.tensor_scalar(onehot[:, slot, j, :], tile_step[:, :], key_t[:, bass.ds(g * UG + j, 1)], None,
                                            ALU.is_equal).then_inc(onehot_made, 1)

            dve.wait_ge(cmask_spread, 1)
            nc.vector.tensor_copy(cmask_T[:, :], ps_cmask).then_inc(carry_step, 1)
            dve.wait_ge(carry_step, 1)
            dve.wait_ge(F_turned, 1)
            nc.vector.tensor_tensor_scan(ct[:, 1:P + 1], cmask_T[:, :], ps_F, 0.0, ALU.min,
                                         ALU.max).then_inc(carry_step, 1)
            onehots(0, 0, UG)
            dve.wait_ge(C_turned, 1)
            nc.vector.tensor_copy(cprev[:, :], ps_C).then_inc(carry_ready, 1)

            def finish_group(g, slot, n):
                dve.wait_ge(out_made, g + 1)
                nc.vector.tensor_tensor(xs[:, bass.ds(g * UG, n), :], ps_out[slot][:, 0:n, :],
                                        xs[:, bass.ds(g * UG, n), :], ALU.add).then_inc(res_made, 1)

            def update_group(g, i, slot, n, n_next, first):
                if n_next:
                    if not first:
                        dve.wait_ge(fix_made, g)
                    onehots(g + 1, 1 - slot, n_next)
                dve.wait_ge(fix_made, g + 1)
                for j in range(n):
                    dve.wait_ge(m_gathered[slot][j], 16 * (i + 1))
                    nc.vector.scalar_tensor_tensor(out=mmax[:, slot, j, :], in0=ps_fix[:, j, :], scalar=drop[:, bass.ds(g * UG + j, 1)],
                                                   in1=gath[:, slot, j, :], op0=ALU.add, op1=ALU.max
                                                   ).then_inc(joined, 1)
                if not first:
                    dve.wait_ge(aggT_made, g)
                for j in range(n):
                    t = g * UG + j
                    dve.wait_ge(joined, t + 1)
                    nc.vector.scalar_tensor_tensor(out=agg[:, slot, j, :], in0=mmax[:, slot, j, :],
                                                   scalar=has[:, bass.ds(t, 1)],
                                                   in1=pm[:, bass.ds(t, 1), :].rearrange("p a f -> p (a f)"),
                                                   op0=ALU.mult, op1=ALU.add).then_inc(agg_made, 1)
                if not first:
                    finish_group(g - 1, 1 - slot, UG)

            dve.wait_ge(count_step, 8)
            update_group(0, 0, 0, UG, UG, True)
            with dve.Fori(0, (NUG - 3) // 2) as i:
                update_group(2 * i + 1, i, 1, UG, UG, False)
                update_group(2 * i + 2, i + 1, 0, UG, UG, False)
            update_group(NUG - 2, (NUG - 3) // 2, 1, UG, LAST_UG, False)
            update_group(NUG - 1, (NUG - 1) // 2, 0, LAST_UG, 0, False)
            finish_group(NUG - 1, 0, LAST_UG)

        @block.tensor
        def _(pe):
            pe.wait_ge(const_made, CONSTS)
            pe.wait_ge(ws_in, 16)

            def turn_group(g, slot):
                for j in range(TG):
                    pe.wait_ge(normed, g * TG + j + 1)
                    last = nc.tensor.transpose(ps_xT[slot][:, j * P:(j + 1) * P], xn[:, slot, j, :], ident[:, :])
                last.then_inc(xT_made, 1)

            def q_group(g, slot, first):
                pe.wait_ge(h_made, g + 1)
                if not first:
                    pe.wait_ge(q_taken, g - 1)
                for j in range(TG):
                    last = nc.tensor.matmul(ps_q[slot][:, j * D:(j + 1) * D], hring[:, slot, j * P:(j + 1) * P],
                                            ws[:, :], start=True, stop=True)
                last.then_inc(q_made, 1)

            turn_group(0, 0)
            q_group(0, 0, True)
            turn_group(1, 1)
            q_group(1, 1, True)
            with pe.Fori(1, NTG // 2) as i:
                turn_group(2 * i, 0)
                q_group(2 * i, 0, False)
                turn_group(2 * i + 1, 1)
                q_group(2 * i + 1, 1, False)
            turn_group(NTG - 1, 0)
            q_group(NTG - 1, 0, False)

            def p_group(g, first):
                pe.wait_ge(h_fixed, g + 1)
                if not first:
                    pe.wait_ge(p_taken, g)
                for j in range(TG):
                    nc.tensor.matmul(ps_p[:, j * D:(j + 1) * D], h_fix[:, j * P:(j + 1) * P], wd[:, :],
                                     start=True, stop=False)
                    last = nc.tensor.matmul(ps_p[:, j * D:(j + 1) * D], ones[0:1, :], bm_row[:, :],
                                            start=False, stop=True)
                last.then_inc(p_made, 1)

            pe.wait_ge(weights_in, 16 * WEIGHTS)
            p_group(0, True)
            with pe.Fori(1, NTG) as g:
                p_group(g, False)

            pe.wait_ge(sel_made, 2)
            nc.tensor.matmul(ps_sel, sel_p[:, :], sel_t[:, :], start=True, stop=True).then_inc(sel_summed, 1)

            def sum_signs(i, slot, first, final):
                pe.wait_ge(signs_made, ((2 * i + slot) + 1) * H)
                for j in range(H):
                    for side in range(2):
                        last = nc.tensor.matmul(ps_count[side], a_sign[:, slot, j, 1 - side:P + 1 - side],
                                                b_sign[:, slot, j, :], start=first and j == 0,
                                                stop=final and j == H - 1)
                last.then_inc(signs_used, 1)

            sum_signs(0, 0, True, False)
            sum_signs(0, 1, False, False)
            with pe.Fori(1, NH // 2 - 1) as i:
                sum_signs(i, 0, False, False)
                sum_signs(i, 1, False, False)
            sum_signs(NH // 2 - 1, 0, False, False)
            sum_signs(NH // 2 - 1, 1, False, True)

            pe.wait_ge(cmask_made, 1)
            nc.tensor.transpose(ps_cmask, cmask[:, :], ident[:, :]).then_inc(cmask_spread, 1)
            pe.wait_ge(edge_step, OPS * SLOTS * LOOPS)
            nc.tensor.transpose(ps_F, runm[:, SLOTS - 1, G - 1, :], ident[:, :]).then_inc(F_turned, 1)
            pe.wait_ge(carry_step, 2)
            nc.tensor.transpose(ps_C, ct[:, 0:P], ident[:, :]).then_inc(C_turned, 1)
            pe.wait_ge(carry_ready, 1)

            def carries(g, slot, n, first=False):
                pe.wait_ge(onehot_made, g * UG + n)
                if not first:
                    pe.wait_ge(joined, g * UG)
                for j in range(n):
                    last = nc.tensor.matmul(ps_fix[:, j, :], onehot[:, slot, j, :], cprev[:, :],
                                            start=True, stop=True)
                last.then_inc(fix_made, 1)

            def out_group(g, slot, n, first):
                pe.wait_ge(hid_kept, g + 1)
                if not first:
                    pe.wait_ge(res_made, g - 1)
                for j in range(n):
                    last = nc.tensor.matmul(ps_out[slot][:, j, :], hidT[:, slot, j * P:(j + 1) * P], w2[:, :],
                                            start=True, stop=True)
                last.then_inc(out_made, 1)

            def update_group(g, slot, n, n_next, wait):
                if n_next:
                    carries(g + 1, 1 - slot, n_next)
                if wait is not None:
                    out_group(g - 1, 1 - slot, UG, wait < 2)
                pe.wait_ge(agg_made, g * UG + n)
                if wait:
                    pe.wait_ge(aggT_kept, g - 1)
                for j in range(n):
                    last = nc.tensor.transpose(ps_aggT[slot][:, j * P:(j + 1) * P], agg[:, slot, j, :], ident[:, :])
                last.then_inc(aggT_made, 1)
                if wait:
                    pe.wait_ge(hid_kept, g - 1)
                nc.tensor.matmul(ps_hid[slot][:, 0:n * P], w1a[:, :], hT[:, bass.ds(g * (UG * P), n * P)],
                                 start=True, stop=False)
                pe.wait_ge(aggT_kept, g + 1)
                nc.tensor.matmul(ps_hid[slot][:, 0:n * P], w1b[:, :], aggT[:, slot, 0:n * P],
                                 start=False, stop=True).then_inc(hid_made, 1)

            carries(0, 0, UG, True)
            update_group(0, 0, UG, UG, None)
            update_group(1, 1, UG, UG, 0)
            update_group(2, 0, UG, UG, 1)
            update_group(3, 1, UG, UG, 2)
            with pe.Fori(2, NUG // 2 - 1) as i:
                update_group(2 * i, 0, UG, UG, 2)
                update_group(2 * i + 1, 1, UG, UG, 2)
            update_group(NUG - 3, 0, UG, UG, 2)
            update_group(NUG - 2, 1, UG, LAST_UG, 2)
            update_group(NUG - 1, 0, LAST_UG, 0, 2)
            out_group(NUG - 1, 0, LAST_UG, False)


_INS = ['x', 'src', 'dst', 'edge_weight', 'L0_gnn_Wm', 'L0_gnn_bm', 'L0_gnn_W1', 'L0_gnn_b1', 'L0_gnn_W2', 'L0_gnn_b2']


def kernel(**inputs):
    import numpy as _np
    import concourse.bacc as _bacc
    from concourse import mybir as _mybir
    from concourse.bass_utils import run_bass_kernel_spmd as _run

    nc = _bacc.Bacc("TRN2", target_bir_lowering=False, num_devices=1)
    pads = {'x': (NN, 0), 'src': (NE, 0), 'dst': (NE, N_NODES), 'edge_weight': (NE, 0)}
    arrays, args = {}, []
    for name in _INS:
        a = _np.ascontiguousarray(inputs[name])
        if name in pads:
            n, value = pads[name]
            padded = _np.full((n,) + a.shape[1:], value, a.dtype)
            padded[:len(a)] = a
            a = padded
        arrays[f"in_{name}_dram"] = a
        args.append(nc.dram_tensor(f"in_{name}_dram", a.shape, _mybir.dt.from_np(a.dtype), kind="ExternalInput").ap())
    q_tab = nc.dram_tensor("q_tab", (NN, D), _mybir.dt.float32, kind="Internal").ap()
    m_tab = nc.dram_tensor("m_tab", (NE, D), _mybir.dt.float32, kind="Internal").ap()
    out = nc.dram_tensor("out_0_dram", (NN, D), _mybir.dt.float32, kind="ExternalOutput").ap()
    build(nc, *args, q_tab, m_tab, out)
    r = _run(nc, [arrays], core_ids=[0])
    return r.results[0]["out_0_dram"][:N_NODES]
```

```python
from contextlib import ExitStack

import concourse.bass as bass
from concourse import mybir

F32 = mybir.dt.float32
I32 = mybir.dt.int32
BF16 = mybir.dt.bfloat16
ALU = mybir.AluOpType
ACT = mybir.ActivationFunctionType

P = 128
D = 128
N_NODES = 6250
N_EDGES = 106250
NT = -(-N_NODES // P)
NN = P * NT
G = 4
SLOTS = 8
PER_LOOP = G * SLOTS
CH = -(-N_EDGES // (P * PER_LOOP)) * PER_LOOP
NE = P * CH
LOOPS = CH // PER_LOOP
HALF = SLOTS // 2
LOOPS_A = LOOPS * 3 // 4
NS = NT + 1
H = 8
NH = CH // H
ROUND = 1.5 * 2.0 ** 23
TG = 7
NTG = NT // TG
POOL_T = TG - 1
POOL_LAST = 4
HS = 4
UG = 4
NUG = -(-NT // UG)
LAST_UG = NT - (NUG - 1) * UG
LIMIT = 3.4028234663852886e38
HUGE = 2.0 ** 127
EPS = 1e-5
OPS = 2 * G
assert PER_LOOP > HS * TG and UG <= G and NT % TG == 0 and NH % 2 == 0 and NUG % 2 == 1 and NTG > 3


def build(nc, x, src, dst, ew, Wm, bm, W1, b1, W2, b2, q_tab, m_tab, out):
    ctx = ExitStack()
    with ctx:
        def sb(name, shape, dt=F32):
            return ctx.enter_context(nc.sbuf_tensor(name, shape, dt))

        def sem(name):
            return ctx.enter_context(nc.semaphore(name))

        xs = sb("xs", [P, NT, D])
        hT = sb("hT", [P, NT * P])
        pm = sb("pm", [P, NT, D])
        dst_sb = sb("dst_sb", [P, CH], I32)
        minus_a = sb("minus_a", [P, CH])
        minus_b = sb("minus_b", [P, CH])
        dst_f = sb("dst_f", [P, CH])
        w_sb = sb("w_sb", [P, CH])
        keep = sb("keep", [P, CH])
        gath = sb("gath", [P, SLOTS, G, D])
        runm = sb("runm", [P, SLOTS, G, D])
        ring_a = gath[:, :, :, :].rearrange("p s j f -> p (s j) f")
        ring_b = runm[:, :, :, :].rearrange("p s j f -> p (s j) f")
        xn = ring_a[:, 0:2 * TG, :].rearrange("p (s t) f -> p s t f", s=2)
        hring = ring_b[:, 0:HS * TG, :].rearrange("p (s t) f -> p s (t f)", s=HS)
        q_sb = ring_a[:, 2 * TG:4 * TG, :].rearrange("p (s t) f -> p s t f", s=2)
        ident = sb("ident", [P, P])
        ws = sb("ws", [P, D])
        wd = sb("wd", [P, D])
        w1a = sb("w1a", [P, D])
        w1b = sb("w1b", [P, D])
        w2 = sb("w2", [P, D])
        ww_b = sb("ww_b", [P, D])
        b2_b = sb("b2_b", [P, D])
        bm_row = sb("bm_row", [1, D])
        h_fix = sb("h_fix", [P, TG * P])
        b1_col = sb("b1_col", [P, 1])
        ones = sb("ones", [P, P])
        a_row = sb("a_row", [P, P + 1])
        b_row = sb("b_row", [P, NS])
        a_sign = sb("a_sign", [P, 2, H, P + 2], BF16)
        b_sign = sb("b_sign", [P, 2, H, NS], BF16)
        count_a = sb("count_a", [P, NS])
        count_b = sb("count_b", [P, NS])
        count_0 = sb("count_0", [P, 1])
        tile_step = sb("tile_step", [P, P])
        minus_t = sb("minus_t", [P, NT])
        src_idx = sb("src_idx", [P, 2, PER_LOOP // 2], I32)
        last_f = sb("last_f", [P, NS])
        last_i = sb("last_i", [P, NS], I32)
        has = sb("has", [P, NT])
        stats = sb("stats", [P, NT, 6])
        mean = sb("mean", [P, NT])
        diff = sb("diff", [P, NT])
        var = sb("var", [P, NT])
        std = sb("std", [P, NT])
        rstd = sb("rstd", [P, NT])
        shift = sb("shift", [P, NT])
        eps_col = sb("eps_col", [P, 1])
        sqrt_eps = sb("sqrt_eps", [P, 1])
        ends = sb("ends", [P, 4], I32)
        ends_f = sb("ends_f", [P, 4])
        flag = sb("flag", [P, 4])
        split_key = sb("split_key", [P, 3])
        key_t = sb("key_t", [P, NT])
        cmask = sb("cmask", [P, P])
        cmask_T = sb("cmask_T", [P, P])
        ct = sb("ct", [P, P + 1])
        cprev = sb("cprev", [P, D])
        drop = sb("drop", [P, NT])
        sel_p = sb("sel_p", [P, P])
        sel_t = sb("sel_t", [P, NT])
        onehot = sb("onehot", [P, 2, UG, P])
        mmax = sb("mmax", [P, 2, UG, D])
        agg = sb("agg", [P, 2, UG, D])
        aggT = sb("aggT", [P, 2, UG * P])
        hidT = sb("hidT", [P, 2, UG * P])

        ps = ctx.enter_context(nc.psum_tensor("ps", [P, 8, 512], F32))
        ps_xT = [ps[:, 2 * i:2 * i + 2, :].rearrange("p b c -> p (b c)") for i in range(2)]
        ps_q = [ps[:, 4 + 2 * i:6 + 2 * i, :].rearrange("p b c -> p (b c)") for i in range(2)]
        ps_p = ps[:, 0:2, :].rearrange("p b c -> p (b c)")
        ps_count = [ps[:, 2 + i, 0:NS] for i in range(2)]
        ps_cmask = ps[:, 4, 0:P]
        ps_F = ps[:, 5, 0:P]
        ps_C = ps[:, 6, 0:P]
        ps_fix = [ps[:, i, :].rearrange("p (j f) -> p j f", f=D) for i in range(2)]
        ps_sel = ps[:, 7, 0:NT]
        ps_aggT = [ps[:, 2 + i, :] for i in range(2)]
        ps_hid = [ps[:, 4 + i, :] for i in range(2)]
        ps_out = [ps[:, 6 + i, :].rearrange("p (j f) -> p j f", f=D) for i in range(2)]

        const_made = sem("const_made")
        ident_zero = sem("ident_zero")
        rows_made = sem("rows_made")
        ends_clear = sem("ends_clear")
        x_in = [sem(f"x_in{g}") for g in range(NTG)]
        weights_in = sem("weights_in")
        ws_in = sem("ws_in")
        ww_in = sem("ww_in")
        edges_in = sem("edges_in")
        ends_in = sem("ends_in")
        split_made = sem("split_made")
        signs_made = sem("signs_made")
        signs_used = sem("signs_used")
        h_fixed = sem("h_fixed")
        p_made = sem("p_made")
        p_taken = sem("p_taken")
        src_idx_in = [sem(f"src_idx_in{i}") for i in range(2)]
        std_made = sem("std_made")
        normed = sem("normed")
        act_normed = sem("act_normed")
        dve_normed = sem("dve_normed")
        xT_made = sem("xT_made")
        h_made = sem("h_made")
        h_kept = [sem(f"h_kept{i}") for i in range(HS)]
        q_made = sem("q_made")
        q_taken = sem("q_taken")
        q_stored = [sem(f"q_stored{i}") for i in range(2)]
        edge_step = sem("edge_step")
        gathered = [sem(f"gathered{i}") for i in range(SLOTS)]
        last_gathered = [sem(f"last_gathered{j}") for j in range(G)]
        m_stored = [sem(f"m_stored{i}") for i in range(SLOTS)]
        cmask_spread = sem("cmask_spread")
        F_turned = sem("F_turned")
        carry_step = sem("carry_step")
        C_turned = sem("C_turned")
        carry_ready = sem("carry_ready")
        onehot_made = sem("onehot_made")
        fix_made = sem("fix_made")
        m_gathered = [[sem(f"m_gathered{s}_{j}") for j in range(UG)] for s in range(2)]
        joined = sem("joined")
        agg_made = sem("agg_made")
        aggT_made = sem("aggT_made")
        aggT_kept = sem("aggT_kept")
        hid_made = sem("hid_made")
        hid_kept = sem("hid_kept")
        out_made = sem("out_made")
        res_made = sem("res_made")
        res_stored = sem("res_stored")
        block = ctx.enter_context(nc.Block())

        stat_step = sem("stat_step")
        var_made = sem("var_made")
        rstd_made = sem("rstd_made")
        shift_made = sem("shift_made")
        prep = sem("prep")
        count_step = sem("count_step")
        cmask_made = sem("cmask_made")
        key_step = sem("key_step")
        sel_made = sem("sel_made")
        sel_summed = sem("sel_summed")
        last_made = sem("last_made")
        m_rows = m_tab.rearrange("(p j) f -> p j f", p=P)
        q_rows = q_tab.rearrange("(p t) f -> p t f", p=P)
        out_rows = out.rearrange("(p t) f -> p t f", p=P)

        def groups_in(slot):
            return len(range(slot, NTG, HS))

        CONSTS = 10
        WEIGHTS = 7
        x_tiles = x.rearrange("(p t) f -> p t f", p=P)
        src_pj = src.rearrange("(p j) -> p j", p=P)
        dst_pj = dst.rearrange("(p j) -> p j", p=P)

        @block.sync
        def _(sp):
            for g in range(NTG):
                sp.dma_start(xs[:, g * TG:(g + 1) * TG, :], x_tiles[:, g * TG:(g + 1) * TG, :]).then_inc(x_in[g], 16)

            def load_indices(i, half):
                sp.dma_start(src_idx[:, half, :],
                             src_pj[:, bass.ds(i * PER_LOOP + half * (PER_LOOP // 2), PER_LOOP // 2)]
                             ).then_inc(src_idx_in[half], 16)

            load_indices(0, 0)
            load_indices(0, 1)
            sp.dma_start(dst_sb[:, :], dst_pj).then_inc(edges_in, 16)
            sp.dma_start(w_sb[:, :], ew.rearrange("(p j) -> p j", p=P)).then_inc(edges_in, 16)

            def keep_h(g):
                sp.wait_ge(h_made, g + 1)
                sp.dma_start(hT[:, g * (TG * P):(g + 1) * (TG * P)], hring[:, g % HS, :]).then_inc(h_kept[g % HS], 16)

            def store_q(g):
                sp.wait_ge(q_taken, g + 1)
                sp.dma_start(q_rows[:, g * TG:(g + 1) * TG, :], q_sb[:, g % 2, :, :]).then_inc(q_stored[g % 2], 16)

            keep_h(0)
            for g in range(NTG):
                if g + 1 < NTG:
                    keep_h(g + 1)
                store_q(g)

            def edge_loop(i, last):
                for s in range(SLOTS):
                    sp.wait_ge(edge_step, i * (OPS * SLOTS) + OPS * (s + 1))
                    sp.dma_start(m_rows[:, bass.ds(i * PER_LOOP + s * G, G), :],
                                 runm[:, s, :, :]).then_inc(m_stored[s], 16)
                    if s % HALF == HALF - 1 and not last:
                        load_indices(i + 1, s // HALF)

            with sp.Fori(0, LOOPS - 1) as i:
                edge_loop(i, False)
            edge_loop(LOOPS - 1, True)

            def update_group(g, n):
                sp.wait_ge(res_made, g + 1)
                sp.dma_start(out_rows[:, bass.ds(g * UG, n), :],
                             xs[:, bass.ds(g * UG, n), :]).then_inc(res_stored, 16)

            with sp.Fori(0, NUG - 1) as g:
                update_group(g, UG)
            update_group(NUG - 1, LAST_UG)
            sp.wait_ge(res_stored, 16 * NUG)

        @block.gpsimd
        def _(pool):
            pool.memset(ones[:, :], 1.0).then_inc(const_made, 1)
            pool.memset(ends[:, :], -1).then_inc(ends_clear, 1)
            pool.iota(a_row[:, :], [[1, P + 1]], base=0, channel_multiplier=0,
                      allow_small_or_imprecise_dtypes=True).then_inc(rows_made, 1)
            pool.iota(b_row[:, :], [[1, NS]], base=0, channel_multiplier=0,
                      allow_small_or_imprecise_dtypes=True).then_inc(rows_made, 1)
            pool.wait_ge(rows_made, 2)
            pool.tensor_scalar(a_row[:, :], a_row[:, :], -0.5, 1.0, ALU.add, ALU.mult).then_inc(const_made, 1)
            pool.tensor_scalar(b_row[:, :], b_row[:, :], -0.5, 1.0, ALU.add, ALU.mult).then_inc(const_made, 1)
            pool.memset(eps_col[:, :], EPS).then_inc(const_made, 1)
            pool.memset(ident[:, :], 0.0).then_inc(ident_zero, 1)
            pool.wait_ge(ident_zero, 1)
            pool.affine_select(out=ident[:, :], in_=ident[:, :], compare_op=ALU.not_equal, fill=1.0, base=0,
                               pattern=[[-1, P]], channel_multiplier=1).then_inc(const_made, 1)
            pool.iota(tile_step[:, :], [[NT, P]], base=0, channel_multiplier=0,
                      allow_small_or_imprecise_dtypes=True).then_inc(const_made, 1)
            pool.iota(minus_t[:, :], [[-1, NT]], base=0, channel_multiplier=0,
                      allow_small_or_imprecise_dtypes=True).then_inc(const_made, 1)
            pool.memset(keep[:, 0:1], -LIMIT).then_inc(const_made, 1)
            pool.memset(runm[:, SLOTS - 1, G - 1, :], 0.0).then_inc(const_made, 1)
            pool.memset(ct[:, 0:1], 0.0).then_inc(const_made, 1)

            for g in range(NTG):
                pool.wait_ge(shift_made, g + 1)
                if g >= 2:
                    pool.wait_ge(xT_made, g - 1)
                for t in range(g * TG, g * TG + (POOL_T if g < NTG - 1 else POOL_LAST)):
                    pool.tensor_scalar(xn[:, g % 2, t % TG, :], xs[:, t, :], rstd[:, t:t + 1], shift[:, t:t + 1],
                                       ALU.mult, ALU.add).then_inc(normed, 1)

            pool.wait_ge(q_stored[0], 16 * (NTG - NTG // 2))
            pool.wait_ge(q_stored[1], 16 * (NTG // 2))

            def gather_group(i, s, last=False):
                pool.wait_ge(src_idx_in[s // HALF], 16 * (i + 1))
                pool.nop(nofuse=True)
                for j in range(G):
                    pool.indirect_dma_start(gath[:, s, j, :], None, q_tab,
                                            bass.IndirectOffsetOnAxis(
                                                src_idx[:, s // HALF, s % HALF * G + j:s % HALF * G + j + 1], 0)
                                            ).then_inc(last_gathered[j] if last else gathered[s], 16)

            for s in range(SLOTS):
                gather_group(0, s)

            def gather_loop(i, last):
                for s in range(SLOTS):
                    pool.wait_ge(edge_step, (i - 1) * (OPS * SLOTS) + OPS * (s + 1))
                    pool.nop(nofuse=True)
                    gather_group(i, s, last and s == SLOTS - 1)

            with pool.Fori(1, LOOPS - 1) as i:
                gather_loop(i, False)
            gather_loop(LOOPS - 1, True)

            for s in range(SLOTS):
                pool.wait_ge(m_stored[s], 16 * LOOPS)
            pool.wait_ge(last_made, 1)
            pool.wait_ge(edge_step, OPS * SLOTS * LOOPS)

            for t in range(NT):
                g, slot, j = t // UG, t // UG % 2, t % UG
                if g >= 2:
                    pool.wait_ge(joined, (g - 2) * UG + j + 1)
                pool.indirect_dma_start(gath[:, slot, j, :], None, m_tab,
                                        bass.IndirectOffsetOnAxis(last_i[:, t + 1:t + 2], 0)
                                        ).then_inc(m_gathered[slot][j], 16)

        @block.scalar
        def _(act):
            act.dma_start(ws[:, :], Wm[D:2 * D, :]).then_inc(ws_in, 16)
            act.dma_start(ww_b[:, :], Wm[2 * D:2 * D + 1, :].broadcast_to([P, D])).then_inc(ww_in, 16)

            act.wait_ge(const_made, CONSTS)
            nc.scalar.activation(sqrt_eps[:, :], eps_col[:, :], ACT.Sqrt)

            def std_group(g):
                act.wait_ge(var_made, g + 1)
                nc.scalar.activation(std[:, g * TG:(g + 1) * TG], var[:, g * TG:(g + 1) * TG], ACT.Sqrt,
                                     bias=eps_col[:, 0:1]).then_inc(std_made, 1)

            def norm_tile(g):
                act.wait_ge(shift_made, g + 1)
                if g >= 2:
                    act.wait_ge(xT_made, g - 1)
                t = g * TG + TG - 1
                nc.scalar.activation(xn[:, g % 2, TG - 1, :], xs[:, t, :], ACT.Identity, bias=shift[:, t:t + 1],
                                     scale=rstd[:, t:t + 1]).then_inc(act_normed, 1)

            def take_h(g):
                slot = g % 2
                act.wait_ge(xT_made, g + 1)
                if g >= HS:
                    act.wait_ge(h_kept[g % HS], 16 * (g // HS))
                    act.wait_ge(q_made, g - HS + 1)
                nc.scalar.activation(hring[:, g % HS, :], ps_xT[slot][:, 0:TG * P], ACT.Relu).then_inc(h_made, 1)

            def take_q(g):
                slot = g % 2
                act.wait_ge(q_made, g + 1)
                if g >= 2:
                    act.wait_ge(q_stored[slot], 16 * (g // 2))
                nc.scalar.copy(q_sb[:, slot, :, :], ps_q[slot][:, 0:TG * D].rearrange("p (t f) -> p t f", f=D)
                               ).then_inc(q_taken, 1)

            for g in range(3):
                std_group(g)
            norm_tile(0)
            norm_tile(1)
            take_h(0)
            for g in range(NTG):
                if g + 3 < NTG:
                    std_group(g + 3)
                if g + 2 < NTG - 1:
                    norm_tile(g + 2)
                if g + 1 < NTG:
                    take_h(g + 1)
                take_q(g)

            with nc.allow_non_contiguous_dma(reason="one entry for each partition"):
                act.dma_start(ends[:, 0:1], dst_pj[:, 0:1]).then_inc(ends_in, 16)
                act.dma_start(ends[:, 1:2], dst_pj[:, CH - 1:CH]).then_inc(ends_in, 16)
                act.dma_start(ends[1:P, 2:3], dst_pj[0:P - 1, CH - 1:CH]).then_inc(ends_in, 16)
                act.dma_start(ends[0:P - 1, 3:4], dst_pj[1:P, 0:1]).then_inc(ends_in, 16)
                act.dma_start(b1_col[:, :], b1.rearrange("(f a) -> f a", a=1)).then_inc(weights_in, 16)
            act.dma_start(wd[:, :], Wm[0:D, :]).then_inc(weights_in, 16)
            act.dma_start(bm_row[:, :], bm.rearrange("(a f) -> a f", a=1)).then_inc(weights_in, 16)
            act.dma_start(b2_b[:, :], b2.rearrange("(a f) -> a f", a=1).broadcast_to([P, D])).then_inc(weights_in, 16)
            act.dma_start(w1a[:, :], W1[0:D, :]).then_inc(weights_in, 16)
            act.dma_start(w1b[:, :], W1[D:2 * D, :]).then_inc(weights_in, 16)
            act.dma_start(w2[:, :], W2).then_inc(weights_in, 16)

            for s in range(HS):
                act.wait_ge(h_kept[s], 16 * groups_in(s))
            with act.Fori(0, NTG) as g:
                nc.scalar.copy(h_fix[:, :], hT[:, bass.ds(g * (TG * P), TG * P)]).then_inc(h_fixed, 1)
                act.wait_ge(p_made, g + 1)
                nc.scalar.copy(pm[:, bass.ds(g * TG, TG), :],
                               ps_p[:, 0:TG * D].rearrange("p (t f) -> p t f", f=D)).then_inc(p_taken, 1)

            act.wait_ge(split_made, 2)

            def signs(i, slot, first):
                if not first:
                    act.wait_ge(signs_used, 2 * i + slot - 1)
                for j in range(H):
                    k = (2 * i + slot) * H + j
                    nc.scalar.activation(a_sign[:, slot, j, 0:P + 1], a_row[:, :], ACT.Sign,
                                         bias=minus_a[:, bass.ds(k, 1)])
                    nc.scalar.activation(b_sign[:, slot, j, :], b_row[:, :], ACT.Sign,
                                         bias=minus_b[:, bass.ds(k, 1)]).then_inc(signs_made, 1)

            signs(0, 0, True)
            signs(0, 1, True)
            with act.Fori(1, NH // 2) as i:
                signs(i, 0, False)
                signs(i, 1, False)

            def update_group(g, slot, n, wait):
                act.wait_ge(aggT_made, g + 1)
                if wait:
                    act.wait_ge(hid_made, g - 1)
                nc.scalar.copy(aggT[:, slot, 0:n * P], ps_aggT[slot][:, 0:n * P]).then_inc(aggT_kept, 1)
                act.wait_ge(hid_made, g + 1)
                if wait:
                    act.wait_ge(out_made, g - 1)
                nc.scalar.activation(hidT[:, slot, 0:n * P], ps_hid[slot][:, 0:n * P], ACT.Relu,
                                     bias=b1_col[:, 0:1]).then_inc(hid_kept, 1)

            update_group(0, 0, UG, False)
            update_group(1, 1, UG, False)
            with act.Fori(1, NUG // 2) as i:
                update_group(2 * i, 0, UG, True)
                update_group(2 * i + 1, 1, UG, True)
            update_group(NUG - 1, 0, LAST_UG, True)

        @block.vector
        def _(dve):
            def stats_group(g, arrived):
                dve.wait_ge(arrived, 16)
                for j in range(TG):
                    nc.vector.bn_stats(stats[:, g * TG + j, :], xs[:, g * TG + j, :]).then_inc(stat_step, 1)
                tiles = slice(g * TG, (g + 1) * TG)
                done = g * (TG + 5)
                dve.wait_ge(stat_step, done + TG)
                nc.vector.tensor_tensor(mean[:, tiles], stats[:, tiles, 1], stats[:, tiles, 4],
                                        ALU.add).then_inc(stat_step, 1)
                nc.vector.tensor_tensor(diff[:, tiles], stats[:, tiles, 1], stats[:, tiles, 4],
                                        ALU.subtract).then_inc(stat_step, 1)
                nc.vector.tensor_tensor(var[:, tiles], stats[:, tiles, 2], stats[:, tiles, 5],
                                        ALU.add).then_inc(stat_step, 1)
                dve.wait_ge(stat_step, done + TG + 2)
                nc.vector.scalar_tensor_tensor(out=diff[:, tiles], in0=diff[:, tiles], scalar=0.25,
                                               in1=diff[:, tiles], op0=ALU.mult, op1=ALU.mult
                                               ).then_inc(stat_step, 1)
                nc.vector.tensor_scalar(mean[:, tiles], mean[:, tiles], 0.5, None, ALU.mult).then_inc(stat_step, 1)
                dve.wait_ge(stat_step, done + TG + 4)
                nc.vector.scalar_tensor_tensor(out=var[:, tiles], in0=var[:, tiles], scalar=1.0 / D,
                                               in1=diff[:, tiles], op0=ALU.mult, op1=ALU.add).then_inc(var_made, 1)

            def rstd_group(g):
                tiles = slice(g * TG, (g + 1) * TG)
                dve.wait_ge(std_made, g + 1)
                nc.vector.reciprocal(rstd[:, tiles], std[:, tiles]).then_inc(rstd_made, 1)
                dve.wait_ge(rstd_made, g + 1)
                nc.vector.scalar_tensor_tensor(out=shift[:, tiles], in0=mean[:, tiles], scalar=-1.0,
                                               in1=rstd[:, tiles], op0=ALU.mult, op1=ALU.mult
                                               ).then_inc(shift_made, 1)

            stats_group(0, x_in[0])
            stats_group(1, x_in[1])
            rstd_group(0)
            stats_group(2, x_in[2])
            rstd_group(1)
            stats_group(3, x_in[3])
            rstd_group(2)
            for g in range(3, NTG):
                if g + 1 < NTG:
                    stats_group(g + 1, x_in[g + 1])
                rstd_group(g)
            dve.wait_ge(xT_made, NTG - 2)
            dve.wait_ge(shift_made, NTG)
            for t in range(NT - TG + POOL_LAST, NT):
                nc.vector.tensor_scalar(xn[:, (NTG - 1) % 2, t % TG, :], xs[:, t, :], rstd[:, t:t + 1],
                                        shift[:, t:t + 1], ALU.mult, ALU.add).then_inc(dve_normed, 1)

            dve.wait_ge(const_made, CONSTS)
            dve.wait_ge(weights_in, 16 * WEIGHTS)
            dve.wait_ge(normed, (NTG - 1) * POOL_T + POOL_LAST)
            dve.wait_ge(act_normed, NTG - 1)
            dve.wait_ge(dve_normed, TG - POOL_LAST)
            nc.vector.tensor_tensor(xs[:, :, :], xs[:, :, :],
                                    b2_b[:, :].rearrange("p (t f) -> p t f", t=1).broadcast_to([P, NT, D]),
                                    ALU.add).then_inc(prep, 1)

            dve.wait_ge(edges_in, 32)
            nc.vector.tensor_tensor(keep[:, 1:CH], dst_sb[:, 1:CH], dst_sb[:, 0:CH - 1],
                                    ALU.is_equal).then_inc(prep, 1)
            dve.wait_ge(ends_in, 64)
            nc.vector.tensor_copy(ends_f[:, :], ends[:, :]).then_inc(prep, 1)
            dve.wait_ge(prep, 2)
            nc.vector.tensor_scalar(keep[:, 1:CH], keep[:, 1:CH], 2.0, -1.0, ALU.mult, ALU.add).then_inc(prep, 1)
            dve.wait_ge(prep, 3)
            nc.vector.tensor_tensor(flag[:, 0:1], ends_f[:, 1:2], ends_f[:, 2:3], ALU.is_equal).then_inc(prep, 1)
            nc.vector.tensor_tensor(flag[:, 1:2], ends_f[:, 0:1], ends_f[:, 2:3], ALU.is_equal).then_inc(prep, 1)
            nc.vector.tensor_tensor(flag[:, 2:3], ends_f[:, 0:1], ends_f[:, 3:4], ALU.not_equal).then_inc(prep, 1)
            dve.wait_ge(prep, 4)
            nc.vector.tensor_scalar(keep[:, 1:CH], keep[:, 1:CH], LIMIT, None, ALU.mult).then_inc(prep, 1)
            dve.wait_ge(prep, 7)
            nc.vector.tensor_tensor(flag[:, 1:2], flag[:, 1:2], flag[:, 2:3], ALU.mult).then_inc(prep, 1)
            nc.vector.tensor_scalar(flag[:, 0:1], flag[:, 0:1], 2.0, -1.0, ALU.mult, ALU.add).then_inc(prep, 1)
            dve.wait_ge(prep, 9)
            nc.vector.scalar_tensor_tensor(out=flag[:, 3:4], in0=ends_f[:, 0:1], scalar=1.0, in1=flag[:, 1:2],
                                           op0=ALU.add, op1=ALU.mult).then_inc(prep, 1)
            dve.wait_ge(prep, 10)
            nc.vector.tensor_scalar(cmask[:, :], ones[:, 0:P], flag[:, 0:1], LIMIT, ALU.mult,
                                    ALU.mult).then_inc(cmask_made, 1)
            dve.wait_ge(prep, 11)
            nc.vector.tensor_scalar(key_t[:, :], minus_t[:, :], flag[:, 3:4], -1.0, ALU.add,
                                    ALU.add).then_inc(prep, 1)

            nc.vector.tensor_scalar(split_key[:, 0:1], flag[:, 3:4], -1.0 - (NT - 1) / 2.0, 1.0 / NT, ALU.add,
                                    ALU.mult).then_inc(key_step, 1)
            dve.wait_ge(key_step, 1)
            nc.vector.tensor_scalar(split_key[:, 1:2], split_key[:, 0:1], ROUND, None, ALU.add).then_inc(key_step, 1)
            dve.wait_ge(key_step, 2)
            nc.vector.tensor_scalar(split_key[:, 2:3], split_key[:, 1:2], -ROUND, float(NT), ALU.add,
                                    ALU.mult).then_inc(key_step, 1)
            dve.wait_ge(key_step, 3)
            nc.vector.tensor_scalar(sel_p[:, :], tile_step[:, :], split_key[:, 2:3], None,
                                    ALU.is_equal).then_inc(sel_made, 1)
            dve.wait_ge(prep, 12)
            nc.vector.tensor_scalar(sel_t[:, :], key_t[:, :], split_key[:, 2:3], None,
                                    ALU.is_equal).then_inc(sel_made, 1)

            nc.vector.tensor_copy(dst_f[:, :], dst_sb[:, :]).then_inc(prep, 1)
            dve.wait_ge(prep, 13)
            nc.vector.tensor_scalar(minus_a[:, :], dst_f[:, :], -(NT - 1) / 2.0, 1.0 / NT, ALU.add,
                                    ALU.mult).then_inc(prep, 1)
            dve.wait_ge(prep, 14)
            nc.vector.tensor_scalar(minus_a[:, :], minus_a[:, :], ROUND, None, ALU.add).then_inc(prep, 1)
            dve.wait_ge(prep, 15)
            nc.vector.tensor_scalar(minus_a[:, :], minus_a[:, :], -ROUND, -1.0, ALU.add,
                                    ALU.mult).then_inc(split_made, 1)
            dve.wait_ge(split_made, 1)
            nc.vector.scalar_tensor_tensor(out=minus_b[:, :], in0=minus_a[:, :], scalar=float(NT), in1=dst_f[:, :],
                                           op0=ALU.mult, op1=ALU.add).then_inc(prep, 1)
            dve.wait_ge(prep, 16)
            nc.vector.tensor_scalar(minus_b[:, :], minus_b[:, :], -1.0, None, ALU.mult).then_inc(split_made, 1)

            dve.wait_ge(ww_in, 16)
            for s in range(HS):
                dve.wait_ge(h_kept[s], 16 * groups_in(s))
            def edge_loop(i, first, last=False):
                for s in range(SLOTS):
                    base = i * (OPS * SLOTS) + OPS * s

                    def message(j):
                        nc.vector.scalar_tensor_tensor(
                            out=gath[:, s, j, :], in0=ww_b[:, :], scalar=w_sb[:, bass.ds(i * PER_LOOP + s * G + j, 1)],
                            in1=gath[:, s, j, :], op0=ALU.mult, op1=ALU.add).then_inc(edge_step, 1)

                    def maximum(j):
                        before = runm[:, s, j - 1, :] if j else runm[:, (s - 1) % SLOTS, G - 1, :]
                        dve.wait_ge(edge_step, base + (2 * j + 1))
                        nc.vector.scalar_tensor_tensor(
                            out=runm[:, s, j, :], in0=before, scalar=keep[:, bass.ds(i * PER_LOOP + s * G + j, 1)],
                            in1=gath[:, s, j, :], op0=ALU.min, op1=ALU.max).then_inc(edge_step, 1)

                    if not first:
                        dve.wait_ge(m_stored[s], 16 * i)
                    if last and s == SLOTS - 1:
                        for j in range(G):
                            dve.wait_ge(last_gathered[j], 16)
                            message(j)
                            maximum(j)
                        continue
                    dve.wait_ge(gathered[s], 16 * G * (i + 1))
                    message(0)
                    for j in range(1, G):
                        message(j)
                        maximum(j - 1)
                    maximum(G - 1)

            edge_loop(0, True)
            with dve.Fori(1, LOOPS_A) as i:
                edge_loop(i, False)

            dve.wait_ge(signs_used, NH)
            nc.vector.tensor_copy(count_a[:, :], ps_count[0]).then_inc(count_step, 1)
            dve.wait_ge(count_step, 1)
            nc.vector.tensor_tensor(count_b[:, :], count_a[:, :], ps_count[1], ALU.subtract).then_inc(count_step, 1)
            nc.vector.tensor_tensor(count_0[:, :], count_a[:, 0:1], ps_count[1][:, 0:1],
                                    ALU.add).then_inc(count_step, 1)
            dve.wait_ge(count_step, 3)
            nc.vector.tensor_scalar(last_f[:, :], count_b[:, :], count_0[:, 0:1], 0.25, ALU.subtract,
                                    ALU.mult).then_inc(count_step, 1)
            dve.wait_ge(count_step, 4)
            nc.vector.tensor_scalar(last_f[:, :], last_f[:, :], NE / 2.0 - 1.0, None, ALU.add).then_inc(count_step, 1)
            dve.wait_ge(count_step, 5)
            nc.vector.tensor_scalar(last_i[:, :], last_f[:, :], 0.0, None, ALU.max).then_inc(last_made, 1)
            nc.vector.tensor_tensor(has[:, :], last_f[:, 1:NS], last_f[:, 0:NT], ALU.is_gt).then_inc(count_step, 1)
            dve.wait_ge(count_step, 6)
            dve.wait_ge(p_taken, NTG)
            nc.vector.tensor_tensor(pm[:, :, :], pm[:, :, :],
                                    has[:, :].rearrange("p (t a) -> p t a", a=1).broadcast_to([P, NT, D]),
                                    ALU.mult).then_inc(count_step, 1)
            dve.wait_ge(sel_summed, 1)
            nc.vector.tensor_scalar(drop[:, :], ps_sel, -1.0, HUGE, ALU.add, ALU.mult).then_inc(count_step, 1)

            with dve.Fori(LOOPS_A, LOOPS - 1) as i:
                edge_loop(i, False)
            edge_loop(LOOPS - 1, False, True)

            def onehots(g, slot, n):
                for j in range(n):
                    nc.vector.tensor_scalar(onehot[:, slot, j, :], tile_step[:, :], key_t[:, bass.ds(g * UG + j, 1)],
                                            None, ALU.is_equal).then_inc(onehot_made, 1)

            dve.wait_ge(cmask_spread, 1)
            nc.vector.tensor_copy(cmask_T[:, :], ps_cmask).then_inc(carry_step, 1)
            dve.wait_ge(carry_step, 1)
            dve.wait_ge(F_turned, 1)
            nc.vector.tensor_tensor_scan(ct[:, 1:P + 1], cmask_T[:, :], ps_F, 0.0, ALU.min,
                                         ALU.max).then_inc(carry_step, 1)
            onehots(0, 0, UG)
            dve.wait_ge(C_turned, 1)
            nc.vector.tensor_copy(cprev[:, :], ps_C).then_inc(carry_ready, 1)

            def finish_group(g, slot, n):
                dve.wait_ge(out_made, g + 1)
                nc.vector.tensor_tensor(xs[:, bass.ds(g * UG, n), :], ps_out[slot][:, 0:n, :],
                                        xs[:, bass.ds(g * UG, n), :], ALU.add).then_inc(res_made, 1)

            def update_group(g, i, slot, n, n_next, first, finish):
                if n_next:
                    if not first:
                        dve.wait_ge(fix_made, g)
                    onehots(g + 1, 1 - slot, n_next)
                dve.wait_ge(fix_made, g + 1)
                for j in range(n):
                    dve.wait_ge(m_gathered[slot][j], 16 * (i + 1))
                    nc.vector.scalar_tensor_tensor(out=mmax[:, slot, j, :], in0=ps_fix[slot][:, j, :],
                                                   scalar=drop[:, bass.ds(g * UG + j, 1)], in1=gath[:, slot, j, :], op0=ALU.add, op1=ALU.max
                                                   ).then_inc(joined, 1)
                if not first:
                    dve.wait_ge(aggT_made, g)
                for j in range(n):
                    t = g * UG + j
                    dve.wait_ge(joined, t + 1)
                    nc.vector.scalar_tensor_tensor(out=agg[:, slot, j, :], in0=mmax[:, slot, j, :],
                                                   scalar=has[:, bass.ds(t, 1)],
                                                   in1=pm[:, bass.ds(t, 1), :].rearrange("p a f -> p (a f)"),
                                                   op0=ALU.mult, op1=ALU.add).then_inc(agg_made, 1)
                if finish:
                    finish_group(g - 2, slot, UG)

            dve.wait_ge(count_step, 8)
            update_group(0, 0, 0, UG, UG, True, False)
            update_group(1, 0, 1, UG, UG, False, False)
            with dve.Fori(1, NUG // 2 - 1) as i:
                update_group(2 * i, i, 0, UG, UG, False, True)
                update_group(2 * i + 1, i, 1, UG, UG, False, True)
            update_group(NUG - 3, NUG // 2 - 1, 0, UG, UG, False, True)
            update_group(NUG - 2, NUG // 2 - 1, 1, UG, LAST_UG, False, True)
            update_group(NUG - 1, NUG // 2, 0, LAST_UG, 0, False, True)
            finish_group(NUG - 2, 1, UG)
            finish_group(NUG - 1, 0, LAST_UG)

        @block.tensor
        def _(pe):
            pe.wait_ge(const_made, CONSTS)

            def keep_busy(n):
                for _ in range(n):
                    nc.tensor.transpose(ps_q[0][:, 0:P], ident[:, :], ident[:, :])

            with pe.Fori(0, 4):
                keep_busy(8)
            pe.wait_ge(ws_in, 16)

            def turn_group(g):
                slot = g % 2
                for j in range(TG):
                    if j < (POOL_T if g < NTG - 1 else POOL_LAST):
                        pe.wait_ge(normed, g * POOL_T + j + 1)
                    elif g < NTG - 1:
                        pe.wait_ge(act_normed, g + 1)
                    else:
                        pe.wait_ge(dve_normed, j - POOL_LAST + 1)
                    last = nc.tensor.transpose(ps_xT[slot][:, j * P:(j + 1) * P], xn[:, slot, j, :], ident[:, :])
                    if g < 2 and j < TG - 1:
                        keep_busy(1)
                last.then_inc(xT_made, 1)

            def q_group(g):
                slot = g % 2
                pe.wait_ge(h_made, g + 1)
                if g >= 2:
                    pe.wait_ge(q_taken, g - 1)
                for j in range(TG):
                    last = nc.tensor.matmul(ps_q[slot][:, j * D:(j + 1) * D], hring[:, g % HS, j * P:(j + 1) * P],
                                            ws[:, :], start=True, stop=True)
                last.then_inc(q_made, 1)

            turn_group(0)
            for g in range(NTG):
                if g + 1 < NTG:
                    turn_group(g + 1)
                q_group(g)

            def p_group(g, first):
                pe.wait_ge(h_fixed, g + 1)
                if not first:
                    pe.wait_ge(p_taken, g)
                for j in range(TG):
                    nc.tensor.matmul(ps_p[:, j * D:(j + 1) * D], h_fix[:, j * P:(j + 1) * P], wd[:, :],
                                     start=True, stop=False)
                    last = nc.tensor.matmul(ps_p[:, j * D:(j + 1) * D], ones[0:1, :], bm_row[:, :],
                                            start=False, stop=True)
                last.then_inc(p_made, 1)

            pe.wait_ge(weights_in, 16 * WEIGHTS)
            p_group(0, True)
            with pe.Fori(1, NTG) as g:
                p_group(g, False)

            pe.wait_ge(sel_made, 2)
            nc.tensor.matmul(ps_sel, sel_p[:, :], sel_t[:, :], start=True, stop=True).then_inc(sel_summed, 1)

            def sum_signs(i, slot, first, final):
                pe.wait_ge(signs_made, ((2 * i + slot) + 1) * H)
                for j in range(H):
                    for side in range(2):
                        last = nc.tensor.matmul(ps_count[side], a_sign[:, slot, j, 1 - side:P + 1 - side],
                                                b_sign[:, slot, j, :], start=first and j == 0,
                                                stop=final and j == H - 1)
                last.then_inc(signs_used, 1)

            sum_signs(0, 0, True, False)
            sum_signs(0, 1, False, False)
            with pe.Fori(1, NH // 2 - 1) as i:
                sum_signs(i, 0, False, False)
                sum_signs(i, 1, False, False)
            sum_signs(NH // 2 - 1, 0, False, False)
            sum_signs(NH // 2 - 1, 1, False, True)

            pe.wait_ge(cmask_made, 1)
            nc.tensor.transpose(ps_cmask, cmask[:, :], ident[:, :]).then_inc(cmask_spread, 1)
            pe.wait_ge(edge_step, OPS * SLOTS * LOOPS)
            nc.tensor.transpose(ps_F, runm[:, SLOTS - 1, G - 1, :], ident[:, :]).then_inc(F_turned, 1)
            pe.wait_ge(carry_step, 2)
            nc.tensor.transpose(ps_C, ct[:, 0:P], ident[:, :]).then_inc(C_turned, 1)
            pe.wait_ge(carry_ready, 1)

            def carries(g, slot, n, first=False):
                pe.wait_ge(onehot_made, g * UG + n)
                if not first:
                    pe.wait_ge(joined, (g - 1) * UG)
                for j in range(n):
                    last = nc.tensor.matmul(ps_fix[slot][:, j, :], onehot[:, slot, j, :], cprev[:, :],
                                            start=True, stop=True)
                last.then_inc(fix_made, 1)

            def out_group(g, slot, n, first):
                pe.wait_ge(hid_kept, g + 1)
                if not first:
                    pe.wait_ge(res_made, g - 1)
                for j in range(n):
                    last = nc.tensor.matmul(ps_out[slot][:, j, :], hidT[:, slot, j * P:(j + 1) * P], w2[:, :],
                                            start=True, stop=True)
                last.then_inc(out_made, 1)

            def update_group(g, slot, n, n_next, wait):
                if n_next:
                    carries(g + 1, 1 - slot, n_next, wait is None)
                pe.wait_ge(agg_made, g * UG + n)
                if wait:
                    pe.wait_ge(aggT_kept, g - 1)
                for j in range(n):
                    last = nc.tensor.transpose(ps_aggT[slot][:, j * P:(j + 1) * P], agg[:, slot, j, :], ident[:, :])
                last.then_inc(aggT_made, 1)
                if wait:
                    pe.wait_ge(hid_kept, g - 1)
                nc.tensor.matmul(ps_hid[slot][:, 0:n * P], w1a[:, :], hT[:, bass.ds(g * (UG * P), n * P)],
                                 start=True, stop=False)
                if wait is not None:
                    out_group(g - 1, 1 - slot, UG, wait < 2)
                pe.wait_ge(aggT_kept, g + 1)
                nc.tensor.matmul(ps_hid[slot][:, 0:n * P], w1b[:, :], aggT[:, slot, 0:n * P],
                                 start=False, stop=True).then_inc(hid_made, 1)

            carries(0, 0, UG, True)
            update_group(0, 0, UG, UG, None)
            update_group(1, 1, UG, UG, 0)
            update_group(2, 0, UG, UG, 1)
            update_group(3, 1, UG, UG, 2)
            with pe.Fori(2, NUG // 2 - 1) as i:
                update_group(2 * i, 0, UG, UG, 2)
                update_group(2 * i + 1, 1, UG, UG, 2)
            update_group(NUG - 3, 0, UG, UG, 2)
            update_group(NUG - 2, 1, UG, LAST_UG, 2)
            update_group(NUG - 1, 0, LAST_UG, 0, 2)
            out_group(NUG - 1, 0, LAST_UG, False)


_INS = ['x', 'src', 'dst', 'edge_weight', 'L0_gnn_Wm', 'L0_gnn_bm', 'L0_gnn_W1', 'L0_gnn_b1', 'L0_gnn_W2', 'L0_gnn_b2']


def kernel(**inputs):
    import numpy as _np
    import concourse.bacc as _bacc
    from concourse import mybir as _mybir
    from concourse.bass_utils import run_bass_kernel_spmd as _run

    nc = _bacc.Bacc("TRN2", target_bir_lowering=False, num_devices=1)
    pads = {'x': (NN, 0), 'src': (NE, 0), 'dst': (NE, N_NODES), 'edge_weight': (NE, 0)}
    arrays, args = {}, []
    for name in _INS:
        a = _np.ascontiguousarray(inputs[name])
        if name in pads:
            n, value = pads[name]
            padded = _np.full((n,) + a.shape[1:], value, a.dtype)
            padded[:len(a)] = a
            a = padded
        arrays[f"in_{name}_dram"] = a
        args.append(nc.dram_tensor(f"in_{name}_dram", a.shape, _mybir.dt.from_np(a.dtype), kind="ExternalInput").ap())
    q_tab = nc.dram_tensor("q_tab", (NN, D), _mybir.dt.float32, kind="Internal").ap()
    m_tab = nc.dram_tensor("m_tab", (NE, D), _mybir.dt.float32, kind="Internal").ap()
    out = nc.dram_tensor("out_0_dram", (NN, D), _mybir.dt.float32, kind="ExternalOutput").ap()
    build(nc, *args, q_tab, m_tab, out)
    r = _run(nc, [arrays], core_ids=[0])
    return r.results[0]["out_0_dram"][:N_NODES]
```
